# Optimizing a Trainium2 kernel written in Bass

```python
import numpy as np
import jax
import jax.numpy as jnp

def _softmax(x, axis=-1):
    return jax.nn.softmax(x, axis=axis)

def _gelu(x):
    return jax.nn.gelu(x, approximate=True)

def _silu(x):
    return jax.nn.silu(x)

def _sigmoid(x):
    return jax.nn.sigmoid(x)

def _layernorm(x, axis=-1, eps=1e-05):
    m = jnp.mean(x, axis=axis, keepdims=True)
    v = jnp.var(x, axis=axis, keepdims=True)
    return (x - m) / jnp.sqrt(v + eps)

def _scatter_add(tgt, idx, src, axis=0):
    return tgt.at[idx].add(src)

def _segment_sum(src, seg, n):
    return jax.ops.segment_sum(src, seg, n)
kernel_name = 'mk_hybrid_d1_jaxref_r8_3efc69'

def setup_inputs(seed: int=0):
    np.random.seed(seed)
    _w = jnp.asarray

    def _L0_attn_a_setup():
        import jax, jax.numpy as jnp
        import numpy as np
        BASE_FREQUENCY = 10000.0
        LRP = 17
        MIN_L = 1.0 - LRP / 100.0
        SDT_L = (BASE_FREQUENCY - MIN_L * BASE_FREQUENCY) * 2.0
        ARM_ATTENTION = 2.0
        HEADS_DIM = 64

        def _nrope(xs, base, angle_range):
            N, T, d = xs.shape
            half = d // 2
            inv_freq = base ** (-jnp.arange(half, dtype=jnp.float32) / half)
            pos = jnp.arange(T, dtype=jnp.float32)
            scale = angle_range / jnp.maximum(T - 1, 1)
            ang = pos[:, None] * inv_freq[None, :] * scale
            cos, sin = (jnp.cos(ang), jnp.sin(ang))
            x1, x2 = (xs[..., :half], xs[..., half:])
            return jnp.concatenate([x1 * cos - x2 * sin, x1 * sin + x2 * cos], axis=-1)
        key = jax.random.key(seed)
        ks = jax.random.split(key, 9)
        B, T, E = (4, 128, 128)
        x = jax.random.normal(ks[0], (B, T, E), dtype=jnp.float32)

        def w(k):
            return jax.random.normal(k, (E, E), dtype=jnp.float32) * 0.02
        z = jnp.zeros((E,), dtype=jnp.float32)
        return {'x': x, 'Wq': w(ks[1]), 'bq': z, 'Wk': w(ks[2]), 'bk': z, 'Wv': w(ks[3]), 'bv': z, 'Wo': w(ks[4]), 'bo': z, 'nrope_freq': jnp.zeros((1,), dtype=jnp.float32)}
    _L0_attn_a_in = _L0_attn_a_setup()

    def _L0_attn_b_setup():
        import jax, jax.numpy as jnp
        import numpy as np
        import math
        HIDDEN = 128
        HEADS = 16
        HEAD = HIDDEN // HEADS
        B, N = (2, 256)
        NEG_INF = -10000.0
        key = jax.random.key(seed)
        k1, k2, k3, k4, k5 = jax.random.split(key, 5)
        s = 1.0 / math.sqrt(HIDDEN)
        return {'encodings': jax.random.normal(k1, (B, N, HIDDEN), dtype=jnp.float32), 'attn_w': jax.random.uniform(k2, (3 * HIDDEN, HIDDEN), minval=-s, maxval=s, dtype=jnp.float32), 'attn_b': jax.random.uniform(k3, (3 * HIDDEN,), minval=-s, maxval=s, dtype=jnp.float32), 'out_w': jax.random.uniform(k4, (HIDDEN, HIDDEN), minval=-s, maxval=s, dtype=jnp.float32), 'out_b': jax.random.uniform(k5, (HIDDEN,), minval=-s, maxval=s, dtype=jnp.float32)}
    _L0_attn_b_in = _L0_attn_b_setup()

    def _L0_ffn_setup():
        import jax, jax.numpy as jnp
        import numpy as np
        D_IN, D_HID = (128, 512)

        def _ternary(key, shape):
            return jax.random.randint(key, shape, -1, 2).astype(jnp.float32)

        def _tlin(x, w, s):
            return jnp.einsum('bsi,oi->bso', x, w) * s
        key = jax.random.key(seed)
        ks = jax.random.split(key, 12)
        inv = lambda fan: 1.0 / np.sqrt(fan).astype(np.float32)
        return {'x': jax.random.normal(ks[0], (4, 256, D_IN), dtype=jnp.float32), 'w1_w': _ternary(ks[1], (D_HID, D_IN)), 'w1_s': jax.random.uniform(ks[2], (D_HID,), dtype=jnp.float32) * inv(D_IN), 'w2_w': _ternary(ks[3], (D_HID, D_IN)), 'w2_s': jax.random.uniform(ks[4], (D_HID,), dtype=jnp.float32) * inv(D_IN), 'h1_w': _ternary(ks[5], (D_HID, D_HID)), 'h1_s': jax.random.uniform(ks[6], (D_HID,), dtype=jnp.float32) * inv(D_HID), 'h2_w': _ternary(ks[7], (D_HID, D_HID)), 'h2_s': jax.random.uniform(ks[8], (D_HID,), dtype=jnp.float32) * inv(D_HID), 'w3_w': _ternary(ks[9], (D_IN, D_HID)), 'w3_s': jax.random.uniform(ks[10], (D_IN,), dtype=jnp.float32) * inv(D_HID)}
    _L0_ffn_in = _L0_ffn_setup()
    _d = {'L0_attn_a_x': _L0_attn_a_in['x'], 'L0_attn_a_Wq': _L0_attn_a_in['Wq'], 'L0_attn_a_bq': _L0_attn_a_in['bq'], 'L0_attn_a_Wk': _L0_attn_a_in['Wk'], 'L0_attn_a_bk': _L0_attn_a_in['bk'], 'L0_attn_a_Wv': _L0_attn_a_in['Wv'], 'L0_attn_a_bv': _L0_attn_a_in['bv'], 'L0_attn_a_Wo': _L0_attn_a_in['Wo'], 'L0_attn_a_bo': _L0_attn_a_in['bo'], 'L0_attn_a_nrope_freq': _L0_attn_a_in['nrope_freq'], 'L0_attn_b_attn_w': _L0_attn_b_in['attn_w'], 'L0_attn_b_attn_b': _L0_attn_b_in['attn_b'], 'L0_attn_b_out_w': _L0_attn_b_in['out_w'], 'L0_attn_b_out_b': _L0_attn_b_in['out_b'], 'L0_ffn_w1_w': _L0_ffn_in['w1_w'], 'L0_ffn_w1_s': _L0_ffn_in['w1_s'], 'L0_ffn_w2_w': _L0_ffn_in['w2_w'], 'L0_ffn_w2_s': _L0_ffn_in['w2_s'], 'L0_ffn_h1_w': _L0_ffn_in['h1_w'], 'L0_ffn_h1_s': _L0_ffn_in['h1_s'], 'L0_ffn_h2_w': _L0_ffn_in['h2_w'], 'L0_ffn_h2_s': _L0_ffn_in['h2_s'], 'L0_ffn_w3_w': _L0_ffn_in['w3_w'], 'L0_ffn_w3_s': _L0_ffn_in['w3_s']}
    _x0 = _d['L0_attn_a_x']
    _d['L0_attn_a_x'] = jax.random.normal(jax.random.fold_in(jax.random.key(seed), 1), (16, 256, 128), dtype=_x0.dtype)
    del _x0
    return _d

def reference(L0_attn_a_x, L0_attn_a_Wq, L0_attn_a_bq, L0_attn_a_Wk, L0_attn_a_bk, L0_attn_a_Wv, L0_attn_a_bv, L0_attn_a_Wo, L0_attn_a_bo, L0_attn_a_nrope_freq, L0_attn_b_attn_w, L0_attn_b_attn_b, L0_attn_b_out_w, L0_attn_b_out_b, L0_ffn_w1_w, L0_ffn_w1_s, L0_ffn_w2_w, L0_ffn_w2_s, L0_ffn_h1_w, L0_ffn_h1_s, L0_ffn_h2_w, L0_ffn_h2_s, L0_ffn_w3_w, L0_ffn_w3_s):

    def _L0_attn_a_ref(x, Wq, bq, Wk, bk, Wv, bv, Wo, bo, nrope_freq):
        import jax, jax.numpy as jnp
        import numpy as np
        BASE_FREQUENCY = 10000.0
        LRP = 17
        MIN_L = 1.0 - LRP / 100.0
        SDT_L = (BASE_FREQUENCY - MIN_L * BASE_FREQUENCY) * 2.0
        ARM_ATTENTION = 2.0
        HEADS_DIM = 64

        def _nrope(xs, base, angle_range):
            N, T, d = xs.shape
            half = d // 2
            inv_freq = base ** (-jnp.arange(half, dtype=jnp.float32) / half)
            pos = jnp.arange(T, dtype=jnp.float32)
            scale = angle_range / jnp.maximum(T - 1, 1)
            ang = pos[:, None] * inv_freq[None, :] * scale
            cos, sin = (jnp.cos(ang), jnp.sin(ang))
            x1, x2 = (xs[..., :half], xs[..., half:])
            return jnp.concatenate([x1 * cos - x2 * sin, x1 * sin + x2 * cos], axis=-1)
        B, T, E = x.shape
        HD = HEADS_DIM
        H = E // HD
        half = HD // 2
        q = (x @ Wq + bq).reshape(B, T, H, HD).transpose(0, 2, 1, 3)
        k = (x @ Wk + bk).reshape(B, T, H, HD).transpose(0, 2, 1, 3)
        v = (x @ Wv + bv).reshape(B, T, H, HD).transpose(0, 2, 1, 3)
        q_content, q_spatial = (q[..., :half], q[..., half:])
        k_content, k_spatial = (k[..., :half], k[..., half:])
        base = jax.nn.sigmoid(nrope_freq[0]) * SDT_L + MIN_L * BASE_FREQUENCY
        rng = ARM_ATTENTION * jnp.pi
        q_spatial = _nrope(q_spatial.reshape(B * H, T, half), base, rng).reshape(B, H, T, half)
        k_spatial = _nrope(k_spatial.reshape(B * H, T, half), base, rng).reshape(B, H, T, half)
        q = jnp.concatenate([q_content, q_spatial], axis=-1)
        k = jnp.concatenate([k_content, k_spatial], axis=-1)
        score = jnp.einsum('bhqd,bhkd->bhqk', q, k) / jnp.sqrt(jnp.float32(HD))
        attn = jax.nn.softmax(score, axis=-1)
        out = jnp.einsum('bhqk,bhkd->bhqd', attn, v)
        out = out.transpose(0, 2, 1, 3).reshape(B, T, E)
        return out @ Wo + bo

    def _L0_attn_b_ref(encodings, attn_w, attn_b, out_w, out_b):
        import jax, jax.numpy as jnp
        import numpy as np
        import math
        HIDDEN = 128
        HEADS = 16
        HEAD = HIDDEN // HEADS
        B, N = (2, 256)
        NEG_INF = -10000.0
        b, n, _ = encodings.shape
        qkv = encodings @ attn_w.T + attn_b
        qkv = qkv.reshape(b, n, HEADS, 3 * HEAD).transpose(0, 2, 1, 3)
        q, k, v = jnp.split(qkv, 3, axis=-1)
        mask = jnp.arange(n)[:, None] <= jnp.arange(n)[None, :]
        scores = jnp.einsum('bhki,bhqi->bhkq', k, q) / math.sqrt(HEAD)
        scores = jnp.where(mask, scores, NEG_INF)
        probs = jax.nn.softmax(scores, axis=2)
        combined = jnp.einsum('bhkq,bhkl->bhql', probs, v)
        out = combined.transpose(0, 2, 1, 3).reshape(b, n, HIDDEN)
        return out @ out_w.T + out_b

    def _L0_ffn_ref(x, w1_w, w1_s, w2_w, w2_s, h1_w, h1_s, h2_w, h2_s, w3_w, w3_s):
        import jax, jax.numpy as jnp
        import numpy as np
        D_IN, D_HID = (128, 512)

        def _ternary(key, shape):
            return jax.random.randint(key, shape, -1, 2).astype(jnp.float32)

        def _tlin(x, w, s):
            return jnp.einsum('bsi,oi->bso', x, w) * s
        h = jax.nn.silu(_tlin(x, w1_w, w1_s)) * _tlin(x, w2_w, w2_s)
        h = jax.nn.gelu(_tlin(h, h1_w, h1_s), approximate=False)
        h = jax.nn.gelu(_tlin(h, h2_w, h2_s), approximate=False)
        return _tlin(h, w3_w, w3_s)
    x = L0_attn_a_x
    x = x + _L0_attn_a_ref(_layernorm(x, axis=-1), L0_attn_a_Wq, L0_attn_a_bq, L0_attn_a_Wk, L0_attn_a_bk, L0_attn_a_Wv, L0_attn_a_bv, L0_attn_a_Wo, L0_attn_a_bo, L0_attn_a_nrope_freq)
    x = x + _L0_ffn_ref(_layernorm(x, axis=-1), L0_ffn_w1_w, L0_ffn_w1_s, L0_ffn_w2_w, L0_ffn_w2_s, L0_ffn_h1_w, L0_ffn_h1_s, L0_ffn_h2_w, L0_ffn_h2_s, L0_ffn_w3_w, L0_ffn_w3_s)
    x = x + _L0_attn_b_ref(_layernorm(x, axis=-1), L0_attn_b_attn_w, L0_attn_b_attn_b, L0_attn_b_out_w, L0_attn_b_out_b)
    x = x + _L0_ffn_ref(_layernorm(x, axis=-1), L0_ffn_w1_w, L0_ffn_w1_s, L0_ffn_w2_w, L0_ffn_w2_s, L0_ffn_h1_w, L0_ffn_h1_s, L0_ffn_h2_w, L0_ffn_h2_s, L0_ffn_w3_w, L0_ffn_w3_s)
    return x

_drawn_inputs = setup_inputs


def setup_inputs(seed=0):
    import zlib

    import numpy as np

    out = dict(_drawn_inputs(seed))
    spreads = {'L0_attn_a_bq': (0.0, 0.1),
     'L0_attn_a_bk': (0.0, 0.1),
     'L0_attn_a_bv': (0.0, 0.1),
     'L0_attn_a_bo': (0.0, 0.1)}
    factors = {}
    for name, (base, spread) in spreads.items():
        noise = np.random.default_rng([zlib.crc32(name.encode()), seed]).standard_normal(out[name].shape)
        drawn = base * np.exp(spread * noise) if base else spread * noise
        out[name] = jnp.asarray(drawn.astype(out[name].dtype))
    for name, factor in factors.items():
        out[name] = (out[name] * factor).astype(out[name].dtype)
    return out
```

```python
from contextlib import ExitStack

import concourse.bass as bass
import numpy as np
from concourse import mybir

F32 = mybir.dt.float32
F32R = mybir.dt.float32r
BF16 = mybir.dt.bfloat16
I32 = mybir.dt.int32
ALU = mybir.AluOpType
ACT = mybir.ActivationFunctionType
AX = mybir.AxisListType

P = 128
B, T, E = 16, 256, 128
SEQS = 2
TOK = SEQS * T
TILES = TOK // P
BLOCKS = B * T // TOK
HID = 512
KC = HID // P
HA, DA = 2, 64
HALF_A = DA // 2
BASE_FREQUENCY, MIN_L = 10000.0, 0.83
SDT_L = (BASE_FREQUENCY - MIN_L * BASE_FREQUENCY) * 2.0
ANGLE_STEP = 2.0 * np.pi / (T - 1)
BELOW_PI = 3.1415925
SCALE_A = DA**-0.5
HB, DB = 16, 8
GROUPS = 4
QUART = P // GROUPS
SCALE_B = DB**-0.5
MASKED = -1e30
EPS = 1e-5

COLS = {}
for _name, _n in (("s1", KC), ("s2", KC), ("h1s", KC), ("h2s", KC), ("bq", 1), ("bqr", 1), ("bk", 1), ("bkr", 1),
                  ("bq_b", 1), ("bk_b", 1), ("freq", 1), ("exponent", 1), ("sign", 1), ("spatial", 1)):
    COLS[_name] = (sum(n for _, n in COLS.values()), _n)
N_COLS = sum(n for _, n in COLS.values())
ROWS = ("bv", "bo", "w3s", "bv_b", "bo_b")


class Block:

    def __init__(self, pair, odd):
        self.pair, self.odd = pair, odd
        self.t = 2 * pair + odd

    def after(self, n):
        return Block(self.pair + (self.odd + n) // 2, (self.odd + n) % 2)


class Stage:

    def __init__(self, sp, act, dve, pool, pe, done=None):
        self.sp, self.act, self.dve, self.pool, self.pe, self.done = sp, act, dve, pool, pe, done


def build(nc, io, layers=("A", "F", "B", "F")):
    ctx = ExitStack()
    with ctx:
        scope = [ctx]

        def sb(name, shape, dt=F32):
            return scope[-1].enter_context(nc.sbuf_tensor(name, shape, dt))

        def sem(name):
            return ctx.enter_context(nc.semaphore(name))

        banks = [ctx.enter_context(nc.psum_tensor(f"bank{i}", [P, 512], F32)) for i in range(5)]
        banks3 = ctx.enter_context(nc.psum_tensor("banks3", [P, 3, 512], F32))

        X = sb("X", [P, B * T // P, E])
        ident = sb("ident", [P, P])
        cols = sb("cols", [P, N_COLS])
        rows = sb("rows", [P, len(ROWS), E])
        stats = sb("stats", [P, TILES, 6])
        mv = sb("mv", [P, TILES, 2])
        veps = sb("veps", [P, TILES])
        rstd = sb("rstd", [P, TILES])
        xn = sb("xn", [P, TILES, E])
        eps_t = sb("eps_t", [P, TILES])
        mhalf = sb("mhalf", [P, TILES])
        xnT = [sb(f"xnT{i}", [P, TOK]) for i in range(2)]

        def col(name, i=0):
            at, _ = COLS[name]
            return cols[:, at + i:at + i + 1]

        def row4(name):
            return rows[:, ROWS.index(name):ROWS.index(name) + 1, :].to_broadcast([P, TILES, E])

        def xblk(t):
            return X[:, bass.ds(TILES * t, TILES), :]

        s_const = sem("constants_ready")
        s_in = sem("tables_loaded")
        s_x0 = sem("x_first_block_loaded")
        s_x1 = sem("x_rest_loaded")
        s_out = sem("output_stored")

        x_dram = io["x"].rearrange("(t p) e -> p t e", p=P)
        out_dram = io["out"].rearrange("(t p) e -> p t e", p=P)

        def sp_load_tables(sp):
            sp.dma_start(cols[:, :], io["cols"]).then_inc(s_in, 16)
            sp.dma_start(X[:, 0:TILES, :], x_dram[:, 0:TILES, :]).then_inc(s_x0, 16)
            sp.dma_start(rows[:, :, :], io["rows"].rearrange("p (r e) -> p r e", e=E)).then_inc(s_in, 16)

        def pool_constants(pool):
            nc.gpsimd.memset(eps_t[:, :], EPS).then_inc(s_const, 1)
            nc.gpsimd.memset(mhalf[:, :], -0.5).then_inc(s_const, 1)
            nc.gpsimd.memset(ident[:, :], 0.0).then_inc(s_const, 1)
            pool.wait_ge(s_const, 3)
            nc.gpsimd.affine_select(out=ident[:, :], in_=ident[:, :], compare_op=ALU.not_equal, fill=1.0,
                                    base=0, pattern=[[-1, P]], channel_multiplier=1).then_inc(s_const, 1)

        CONSTANTS = 4

        class Norm:

            def __init__(self, layer):
                self.stats = sem(f"{layer}_ln_stats")
                self.moments = sem(f"{layer}_ln_moments")
                self.veps = sem(f"{layer}_ln_variance_eps")
                self.rstd = sem(f"{layer}_ln_rstd")
                self.xn = sem(f"{layer}_xn_ready")
                self.read = sem(f"{layer}_xn_transposed")

            def dve(self, dve, b, first):
                t = b.t
                for s in range(TILES):
                    nc.vector.bn_stats(stats[:, s, :], X[:, bass.ds(TILES * t + s, 1), :]).then_inc(self.stats, 1)
                dve.drain()
                for s in range(TILES):
                    nc.vector.bn_aggr(mv[:, s, :], stats[:, s, :]).then_inc(self.moments, 1)
                dve.wait_ge(self.rstd, t + 1)
                if not first:
                    dve.wait_ge(self.read, t)
                for s in range(TILES):
                    nc.vector.tensor_scalar(xn[:, s, :], X[:, bass.ds(TILES * t + s, 1), :], mv[:, s, 0:1],
                                            rstd[:, s:s + 1], ALU.subtract, ALU.mult).then_inc(self.xn, 1)

            def pool(self, pool, b):
                t = b.t
                pool.wait_ge(self.moments, TILES * (t + 1))
                nc.gpsimd.tensor_tensor(veps[:, :], mv[:, :, 1], eps_t[:, :], ALU.add).then_inc(self.veps, 1)
                pool.wait_ge(self.veps, t + 1)
                pool.wait_ge(self.xn, TILES * t)
                nc.gpsimd.tensor_tensor(rstd[:, :], veps[:, :], mhalf[:, :], ALU.pow).then_inc(self.rstd, 1)

            def pe(self, pe, b, bank):
                pe.wait_ge(self.xn, TILES * (b.t + 1))
                for s in range(TILES):
                    last = nc.tensor.transpose(bank[:, s * P:(s + 1) * P], xn[:, s, :], ident[:, :])
                last.then_inc(self.read, 1)

        def mm(out, lhsT, rhs, start=True, stop=True):
            return nc.tensor.matmul(out, lhsT, rhs, start=start, stop=stop)

        def project(bank, w, xT):
            return mm(bank[:, :], w, xT)

        def token_major(bank, xT, w):
            for s in range(TILES):
                last = mm(bank[:, s * P:(s + 1) * P], xT[:, s * P:(s + 1) * P], w)
            return last

        def tiles_of(bank):
            return bank[:, :].rearrange("p (s e) -> p s e", s=TILES)

        def wait(engine, semaphore, value):
            if not isinstance(value, int) or value > 0:
                engine.wait_ge(semaphore, value)

        def run_odd(engine, body):
            body(engine, Block(0, 0), False, True)
            with engine.Fori(0, BLOCKS // 2 - 1) as i:
                body(engine, Block(i, 1), True, True)
                body(engine, Block(i + 1, 0), True, True)
            body(engine, Block(BLOCKS // 2 - 1, 1), True, False)

        def attention_a(x_ready_before):
            wA = sb("wA", [P, 6, E])
            WQ, WQR, WK, WKR, WV, WO = range(6)
            C = sb("cosines", [P, T])
            S = sb("sines", [P, T])
            qT = [sb(f"a_qT{i}", [P, TOK]) for i in range(2)]
            kT = [sb(f"a_kT{i}", [P, TOK]) for i in range(2)]
            v = [sb(f"a_v{i}", [P, TILES, E]) for i in range(2)]
            turned = sb("a_turned", [P, TOK])
            straight = sb("a_straight", [P, TOK])
            prob = [sb(f"a_prob{i}", [P, 2, T]) for i in range(2)]
            probT = [sb(f"a_probT{i}", [P, 2, T]) for i in range(2)]
            mx = [sb(f"a_mx{i}", [P, 2]) for i in range(2)]
            nm = [sb(f"a_nm{i}", [P, 2]) for i in range(2)]
            total = [sb(f"a_total{i}", [P, 2]) for i in range(2)]
            inv = [sb(f"a_inv{i}", [P, 2]) for i in range(2)]
            oT = sb("a_oT", [P, TOK])
            tab = [sb(f"a_tab{i}", [P, T]) for i in range(4)]
            tcol = sb("a_tcol", [P, 8])
            posi = sb("a_posi", [P, T], I32)

            misc = banks[0:2]
            score = banks[2:4]
            pT_bank = [banks[4], banks3[:, 0, :]]
            o_bank = banks3[:, 1, :]
            y_bank = banks3[:, 2, :]

            norm = Norm("a")
            s_w = sem("a_weights_loaded")
            s_tab = sem("a_table_steps_pool")
            s_tabd = sem("a_table_steps_dve")
            s_taba = sem("a_table_steps_act")
            s_tr = sem("a_rope_tables_ready")
            s_xT = sem("a_xnT_ready")
            s_q = sem("a_q_product")
            s_qr = sem("a_q_rotated_product")
            s_k = sem("a_k_product")
            s_kr = sem("a_k_rotated_product")
            s_v = sem("a_v_product")
            s_st = sem("a_rope_straight")
            s_tu = sem("a_rope_turned")
            s_ro = sem("a_rope_added")
            s_vr = sem("a_v_ready")
            s_sc = sem("a_scores")
            s_mx = sem("a_max")
            s_nm = sem("a_negative_max")
            s_ex = sem("a_exponentials")
            s_in_ = sem("a_inverse_total")
            s_no = sem("a_probabilities_normalised")
            s_pt = sem("a_probabilities_transposed")
            s_pc = sem("a_probabilities_copied")
            s_pv = sem("a_values_weighted")
            s_oc = sem("a_outputs_copied")
            s_y = sem("a_projected")
            s_bo = sem("a_bias_added_to_x")
            s_done = sem("a_x_updated")

            def sp_program(sp):
                sp.dma_start(wA[:, :, :], io["wA"].rearrange("p (w e) -> p w e", e=E)).then_inc(s_w, 16)
                sp.dma_start(X[:, TILES:, :], x_dram[:, TILES:, :]).then_inc(s_x1, 16)

            UNITS = SEQS * HA

            def unit(n):
                return n // HA, n % HA

            def pool_tables(pool):
                nc.gpsimd.iota(posi[:, :], pattern=[[1, T]], base=0, channel_multiplier=0).then_inc(s_tab, 1)
                pool.wait_ge(s_in, 32)
                pool.wait_ge(s_tabd, 3)
                nc.gpsimd.tensor_tensor(tcol[:, 3:4], tcol[:, 2:3], col("exponent"), ALU.pow).then_inc(s_tab, 1)

            def act_tables(act):
                act.wait_ge(s_in, 32)
                nc.scalar.activation(tcol[:, 0:1], col("freq"), ACT.Exp, scale=-1.0).then_inc(s_taba, 1)
                act.wait_ge(s_tabd, 6)
                nc.scalar.activation(tab[1][:, :], tab[0][:, :], ACT.Sin).then_inc(s_taba, 1)
                nc.scalar.activation(tab[2][:, :], tab[3][:, :], ACT.Sin).then_inc(s_taba, 1)

            def dve_tables(dve):
                dve.wait_ge(s_taba, 1)
                nc.vector.tensor_scalar_add(tcol[:, 1:2], tcol[:, 0:1], 1.0).then_inc(s_tabd, 1)
                dve.wait_ge(s_tabd, 1)
                nc.vector.reciprocal(tcol[:, 4:5], tcol[:, 1:2]).then_inc(s_tabd, 1)
                dve.wait_ge(s_tabd, 2)
                nc.vector.tensor_scalar(tcol[:, 2:3], tcol[:, 4:5], SDT_L, MIN_L * BASE_FREQUENCY,
                                        ALU.mult, ALU.add).then_inc(s_tabd, 1)
                dve.wait_ge(s_tab, 2)
                nc.vector.tensor_copy(tab[1][:, :], posi[:, :]).then_inc(s_tabd, 1)
                dve.wait_ge(s_tabd, 4)
                nc.vector.tensor_scalar(tab[2][:, :], tab[1][:, :], tcol[:, 3:4], float(ANGLE_STEP / 2),
                                        ALU.mult, ALU.mult).then_inc(s_tabd, 1)
                dve.wait_ge(s_tabd, 5)
                nc.vector.tensor_scalar_min(tab[0][:, :], tab[2][:, :], BELOW_PI)
                nc.vector.tensor_scalar(tab[3][:, :], tab[2][:, :], -1.0, float(np.pi / 2),
                                        ALU.mult, ALU.add).then_inc(s_tabd, 1)
                dve.wait_ge(s_taba, 3)
                nc.vector.tensor_tensor(tab[0][:, :], tab[1][:, :], tab[2][:, :], ALU.mult).then_inc(s_tabd, 1)
                nc.vector.tensor_tensor(tab[3][:, :], tab[1][:, :], tab[1][:, :], ALU.mult).then_inc(s_tabd, 1)
                dve.wait_ge(s_tabd, 8)
                nc.vector.tensor_scalar(S[:, :], tab[0][:, :], col("sign"), 2.0, ALU.mult, ALU.mult).then_inc(s_tr, 1)
                nc.vector.tensor_scalar(tab[1][:, :], tab[3][:, :], col("spatial"), -2.0,
                                        ALU.mult, ALU.mult).then_inc(s_tabd, 1)
                dve.wait_ge(s_tabd, 9)
                nc.vector.tensor_scalar_add(C[:, :], tab[1][:, :], 1.0).then_inc(s_tr, 1)

            def pe_T(pe, n):
                pe.wait_ge(s_ro, 2 * n.t)
                norm.pe(pe, n, misc[0])

            def pe_proj(pe, n, which):
                t = n.t
                xT = xnT[n.odd][:, :]
                if which == "q":
                    pe.wait_ge(s_xT, t + 1)
                    pe.wait_ge(s_vr, t)
                    project(misc[1], wA[:, WQ, :], xT).then_inc(s_q, 1)
                elif which == "qr":
                    project(misc[0], wA[:, WQR, :], xT).then_inc(s_qr, 1)
                elif which == "k":
                    pe.wait_ge(s_st, 2 * t + 1)
                    project(misc[1], wA[:, WK, :], xT).then_inc(s_k, 1)
                elif which == "kr":
                    pe.wait_ge(s_tu, 2 * t + 1)
                    project(misc[0], wA[:, WKR, :], xT).then_inc(s_kr, 1)
                elif which == "v":
                    pe.wait_ge(s_st, 2 * t + 2)
                    token_major(misc[1], xT, wA[:, WV, :]).then_inc(s_v, 1)

            def pe_scores(pe, b, n):
                s, h = unit(n)
                if n:
                    wait(pe, s_ex, UNITS * b.t + n - 1)
                else:
                    pe.wait_ge(s_ro, 2 * (b.t + 1))
                at = slice(64 * h, 64 * h + 64)
                for qt in range(2):
                    last = mm(score[n % 2][:, qt * T:(qt + 1) * T],
                              qT[b.odd][at, s * T + qt * P:s * T + (qt + 1) * P],
                              kT[b.odd][at, s * T:(s + 1) * T])
                last.then_inc(s_sc, 1)

            def pe_probT(pe, b, n):
                pe.wait_ge(s_no, UNITS * b.t + n + 1)
                if n >= 2:
                    pe.wait_ge(s_pc, UNITS * b.t + n - 1)
                for kc in range(2):
                    for qt in range(2):
                        last = nc.tensor.transpose(pT_bank[n % 2][:, kc * T + qt * P:kc * T + (qt + 1) * P],
                                                   prob[n % 2][:, qt, kc * P:(kc + 1) * P], ident[:, :])
                last.then_inc(s_pt, 1)

            def pe_pv(pe, b, n):
                s, h = unit(n)
                pe.wait_ge(s_pc, UNITS * b.t + n + 1)
                if n == 0:
                    pe.wait_ge(s_oc, b.t)
                    pe.wait_ge(s_vr, b.t + 1)
                for kc in range(2):
                    last = mm(o_bank[64 * h:64 * h + 64, s * T:(s + 1) * T],
                              v[b.odd][:, 2 * s + kc, 64 * h:64 * h + 64], probT[n % 2][:, kc, :],
                              start=kc == 0, stop=kc == 1)
                last.then_inc(s_pv, 1)

            def pe_out(pe, b):
                pe.wait_ge(s_oc, b.t + 1)
                pe.wait_ge(s_done, b.t)
                token_major(y_bank, oT, wA[:, WO, :]).then_inc(s_y, 1)

            def pe_body(pe, b, before, more):
                n = b.after(1)
                pe_scores(pe, b, 0)
                pe_scores(pe, b, 1)
                pe_probT(pe, b, 0)
                if more:
                    pe_T(pe, n)
                pe_scores(pe, b, 2)
                pe_probT(pe, b, 1)
                pe_pv(pe, b, 0)
                if more:
                    pe_proj(pe, n, "q")
                pe_scores(pe, b, 3)
                if more:
                    pe_proj(pe, n, "qr")
                pe_probT(pe, b, 2)
                pe_pv(pe, b, 1)
                if more:
                    pe_proj(pe, n, "k")
                pe_probT(pe, b, 3)
                pe_pv(pe, b, 2)
                if more:
                    pe_proj(pe, n, "kr")
                pe_pv(pe, b, 3)
                if more:
                    pe_proj(pe, n, "v")
                pe_out(pe, b)

            def pe_program(pe):
                pe.wait_ge(s_const, CONSTANTS)
                pe.wait_ge(s_w, 16)
                first = Block(0, 0)
                norm.pe(pe, first, misc[0])
                for which in ("q", "qr", "k", "kr", "v"):
                    pe_proj(pe, first, which)
                run_odd(pe, pe_body)

            def act_xT(act, n):
                act.wait_ge(norm.read, n.t + 1)
                nc.scalar.activation(xnT[n.odd][:, :], misc[0][:, :], ACT.Copy).then_inc(s_xT, 1)

            def act_exp(act, b, n):
                act.wait_ge(s_nm, UNITS * b.t + n + 1)
                if n >= 2:
                    act.wait_ge(s_pt, UNITS * b.t + n - 1)
                for qt in range(2):
                    last = nc.scalar.activation(prob[n % 2][:, qt, :], score[n % 2][:, qt * T:(qt + 1) * T], ACT.Exp,
                                                bias=nm[n % 2][:, qt:qt + 1], scale=SCALE_A,
                                                accum_out=total[n % 2][:, qt:qt + 1])
                last.then_inc(s_ex, 1)

            def act_probT(act, b, n):
                act.wait_ge(s_pt, UNITS * b.t + n + 1)
                if n >= 2:
                    act.wait_ge(s_pv, UNITS * b.t + n - 1)
                nc.scalar.activation(probT[n % 2][:, :, :], pT_bank[n % 2][:, :].rearrange("p (k q) -> p k q", k=2),
                                     ACT.Copy).then_inc(s_pc, 1)

            def act_body(act, b, before, more):
                act_exp(act, b, 0)
                act_exp(act, b, 1)
                act_probT(act, b, 0)
                if more:
                    act_xT(act, b.after(1))
                act_exp(act, b, 2)
                act_probT(act, b, 1)
                act_exp(act, b, 3)
                act_probT(act, b, 2)
                act_probT(act, b, 3)

            def act_program(act):
                act_xT(act, Block(0, 0))
                nc.scalar.preload_act_table(ACT.Exp)
                run_odd(act, act_body)

            def as_seqs(ap):
                return ap.rearrange("p (s t) -> p s t", s=SEQS)

            def dve_rope(dve, n, which):
                t = n.t
                k = which in ("k", "kr")
                if which in ("q", "k"):
                    dve.wait_ge(s_k if k else s_q, t + 1)
                    dve.wait_ge(s_ro, 2 * t + k)
                    nc.vector.scalar_tensor_tensor(
                        out=as_seqs(straight[:, :]), in0=as_seqs(misc[1][:, :]), scalar=col("bk" if k else "bq"),
                        in1=C[:, :].unsqueeze(1).to_broadcast([P, SEQS, T]), op0=ALU.add, op1=ALU.mult).then_inc(s_st, 1)
                else:
                    dve.wait_ge(s_kr if k else s_qr, t + 1)
                    nc.vector.scalar_tensor_tensor(
                        out=as_seqs(turned[:, :]), in0=as_seqs(misc[0][:, :]), scalar=col("bkr" if k else "bqr"),
                        in1=S[:, :].unsqueeze(1).to_broadcast([P, SEQS, T]), op0=ALU.add, op1=ALU.mult).then_inc(s_tu, 1)

            def dve_v(dve, n):
                dve.wait_ge(s_v, n.t + 1)
                nc.vector.tensor_tensor(v[n.odd][:, :, :], tiles_of(misc[1]), row4("bv"), ALU.add).then_inc(s_vr, 1)

            def dve_max(dve, b, n):
                dve.wait_ge(s_sc, UNITS * b.t + n + 1)
                nc.vector.reduce_max(mx[n % 2][:, :], score[n % 2][:, :].rearrange("p (q k) -> p q k", q=2),
                                     AX.X).then_inc(s_mx, 1)
                dve.wait_ge(s_mx, UNITS * b.t + n + 1)
                nc.vector.tensor_scalar_mul(nm[n % 2][:, :], mx[n % 2][:, :], -SCALE_A).then_inc(s_nm, 1)

            def dve_normalise(dve, b, n):
                dve.wait_ge(s_ex, UNITS * b.t + n + 1)
                nc.vector.reciprocal(inv[n % 2][:, :], total[n % 2][:, :]).then_inc(s_in_, 1)
                dve.wait_ge(s_in_, UNITS * b.t + n + 1)
                for qt in range(2):
                    last = nc.vector.tensor_scalar_mul(prob[n % 2][:, qt, :], prob[n % 2][:, qt, :],
                                                       inv[n % 2][:, qt:qt + 1])
                last.then_inc(s_no, 1)

            def dve_body(dve, b, before, more):
                n = b.after(1)
                if more:
                    norm.dve(dve, n, False)
                dve_max(dve, b, 0)
                dve_max(dve, b, 1)
                dve_normalise(dve, b, 0)
                dve_max(dve, b, 2)
                dve_normalise(dve, b, 1)
                if more:
                    dve_rope(dve, n, "q")
                dve_max(dve, b, 3)
                dve_normalise(dve, b, 2)
                if more:
                    dve_rope(dve, n, "qr")
                    dve_rope(dve, n, "k")
                dve_normalise(dve, b, 3)
                if more:
                    dve_rope(dve, n, "kr")
                dve.wait_ge(s_pv, UNITS * (b.t + 1))
                dve.wait_ge(s_y, b.t)
                nc.vector.tensor_copy(oT[:, :], o_bank[:, :]).then_inc(s_oc, 1)
                if more:
                    dve_v(dve, n)
                dve.wait_ge(s_y, b.t + 1)
                dve.wait_ge(s_bo, b.t + 1)
                nc.vector.tensor_tensor(xblk(b.t), tiles_of(y_bank), xblk(b.t), ALU.add).then_inc(s_done, 1)

            def dve_program(dve):
                first = Block(0, 0)
                dve.wait_ge(s_x0, 16)
                norm.dve(dve, first, True)
                dve.wait_ge(s_tr, 2)
                for which in ("q", "qr", "k", "kr"):
                    dve_rope(dve, first, which)
                dve_v(dve, first)
                dve.wait_ge(s_x1, 16)
                run_odd(dve, dve_body)

            def pool_rope(pool, n):
                t = n.t
                for k, (out, have) in enumerate(((qT, 1), (kT, 2))):
                    pool.wait_ge(s_st, 2 * t + have)
                    pool.wait_ge(s_tu, 2 * t + have)
                    nc.gpsimd.tensor_tensor(out[n.odd][:, :], straight[:, :], turned[:, :], ALU.add).then_inc(s_ro, 1)

            def pool_body(pool, b, before, more):
                if more:
                    norm.pool(pool, b.after(1))
                nc.gpsimd.tensor_tensor(xblk(b.t), xblk(b.t), row4("bo"), ALU.add).then_inc(s_bo, 1)
                if more:
                    pool_rope(pool, b.after(1))

            def pool_program(pool):
                first = Block(0, 0)
                norm.pool(pool, first)
                pool_rope(pool, first)
                run_odd(pool, pool_body)

            return Stage(done=s_done, sp=[sp_program], act=[act_tables, act_program],
                                   dve=[dve_tables, dve_program], pool=[pool_tables, pool_program], pe=[pe_program])

        ffn = {}

        def ffn_weights():
            WCOLS = 2 * HID + 2 * KC * HID + KC * E
            whi = sb("whi", [P, WCOLS], F32R)
            wlo = sb("wlo", [P, WCOLS], F32R)
            piece = 704
            stage = sb("w_stage", [P, 2, piece])
            s_w = [sem(f"f_weights_loaded{i}") for i in range(2)]
            s_hi = sem("f_weights_hi")
            s_lo = sem("f_weights_lo")
            sc = sb("f_scales", [P, 2, KC])
            s_sc = sem("f_scales_ready")
            n = WCOLS // piece

            def sp_split(sp):
                for i in range(n):
                    if i >= 2:
                        sp.wait_ge(s_lo, i - 1)
                    sp.dma_start(stage[:, i % 2, :], io["wF"][:, i * piece:(i + 1) * piece]).then_inc(s_w[i % 2], 16)

            def pool_split(pool):
                for i in range(n):
                    at = slice(i * piece, (i + 1) * piece)
                    pool.wait_ge(s_hi, i + 1)
                    nc.gpsimd.tensor_tensor(wlo[:, at], stage[:, i % 2, :], whi[:, at].bitcast(F32),
                                            ALU.subtract).then_inc(s_lo, 1)

            def act_split(act):
                for i in range(n):
                    act.wait_ge(s_w[i % 2], 16 * (i // 2 + 1))
                    nc.scalar.activation(whi[:, i * piece:(i + 1) * piece], stage[:, i % 2, :],
                                         ACT.Copy).then_inc(s_hi, 1)

            def dve_split(dve):
                dve.wait_ge(s_in, 32)
                s1, s2 = COLS["s1"][0], COLS["s2"][0]
                nc.vector.tensor_scalar_mul(sc[:, 0, :], cols[:, s1:s1 + KC], 0.5).then_inc(s_sc, 1)
                dve.wait_ge(s_sc, 1)
                nc.vector.tensor_tensor(sc[:, 1, :], sc[:, 0, :], cols[:, s2:s2 + KC], ALU.mult).then_inc(s_sc, 1)

            ffn.update(whi=whi, wlo=wlo, s_lo=s_lo, n=n, sc=sc, s_sc=s_sc)
            at = 0
            for name, k, m in (("w1", 1, HID), ("w2", 1, HID), ("h1", KC, HID), ("h2", KC, HID), ("w3", KC, E)):
                ffn[name] = [w[:, at:at + k * m].rearrange("p (k m) -> p k m", k=k) for w in (whi, wlo)]
                at += k * m
            return Stage(sp=[sp_split], act=[act_split], dve=[dve_split], pool=[pool_split], pe=[])

        def feed_forward(layer, x_before):
            F = layer
            ffn["xn"] = [[sb(f"{F}_xn_{part}{i}", [P, TOK], F32R) for i in range(2)] for part in ("hi", "lo")]
            ffn["h"] = [sb(f"{F}_h_{part}", [P, KC, TOK], F32R) for part in ("hi", "lo")]
            ffn["g1"] = [sb(f"{F}_g1_{part}", [P, KC, TOK], F32R) for part in ("hi", "lo")]
            ffn["g2"] = [sb(f"{F}_g2_{part}", [P, KC, TOK], F32R) for part in ("hi", "lo")]
            ffn["th"] = [sb(f"{F}_tanh{i}", [P, TOK]) for i in range(2)]
            ffn["u"] = [sb(f"{F}_gate{i}", [P, TOK]) for i in range(2)]
            ffn["hf"] = [sb(f"{F}_hidden{i}", [P, TOK]) for i in range(2)]
            ffn["gf"] = [sb(f"{F}_gelu{i}", [P, TOK]) for i in range(2)]
            ffn["y"] = sb(f"{F}_y", [P, TILES, E])
            norm = Norm(F)
            xhi, xlo = ffn["xn"]
            hhi, hlo = ffn["h"]
            g1hi, g1lo = ffn["g1"]
            g2hi, g2lo = ffn["g2"]
            th, uu, hf, gf, y, sc = (ffn[k] for k in ("th", "u", "hf", "gf", "y", "sc"))
            t_bank = banks[0]
            a_bank, b_bank = banks[1:3], banks[3:5]
            z_bank = [banks3[:, 0, :], banks3[:, 1, :]]
            y_bank = banks3[:, 2, :]
            s_xhi = sem(f"{F}_xn_hi")
            s_xlo = sem(f"{F}_xn_lo")
            s_ab = sem(f"{F}_gate_products")
            s_th = sem(f"{F}_tanh")
            s_u = sem(f"{F}_gate")
            s_hf = [sem(f"{F}_hidden{i}") for i in range(2)]
            s_hhi = sem(f"{F}_hidden_hi")
            s_hlo = [sem(f"{F}_hidden_lo{i}") for i in range(2)]
            s_z = sem(f"{F}_products")
            s_gf = sem(f"{F}_gelu")
            s_ghi = [sem(f"{F}_gelu_hi{i}") for i in range(2)]
            s_glo = [sem(f"{F}_gelu_lo{i}") for i in range(2)]
            s_y = sem(f"{F}_projected")
            s_ys = sem(f"{F}_scaled")
            s_done = sem(f"{F}_x_updated")

            def product(out, w, x, kcs, sl):
                terms = [(w[i][:, kc, sl], x[j][kc]) for kc in range(kcs) for i, j in ((0, 0), (0, 1), (1, 0))]
                for n, (l, r) in enumerate(terms):
                    last = mm(out, l, r, start=n == 0, stop=n == len(terms) - 1)
                return last

            def pe_gates(pe, n):
                t = n.t
                pe.wait_ge(s_xlo, t + 1)
                pe.wait_ge(s_xhi, t + 1)
                x = [[xhi[n.odd][:, :]], [xlo[n.odd][:, :]]]
                for c in range(KC):
                    if c >= 2:
                        pe.wait_ge(s_hf[c % 2], 2 * t + c // 2)
                    sl = slice(c * P, (c + 1) * P)
                    product(a_bank[c % 2][:, :], ffn["w1"], x, 1, sl)
                    product(b_bank[c % 2][:, :], ffn["w2"], x, 1, sl).then_inc(s_ab, 1)

            def pe_hidden(pe, b, second, middle=None):
                t = b.t
                x = (g1hi, g1lo) if second else (hhi, hlo)
                w = ffn["h2" if second else "h1"]
                ready = s_glo if second else s_hlo
                for slot in range(2):
                    pe.wait_ge(ready[slot], 4 * t + 2 if second else 2 * t + 2)
                x = [[x[j][:, kc, :] for kc in range(KC)] for j in range(2)]
                for c in range(KC):
                    if c == 2 and middle:
                        middle()
                    pe.wait_ge(s_ghi[c % 2], 4 * t + 2 * second + c // 2)
                    product(z_bank[c % 2], w, x, KC, slice(c * P, (c + 1) * P)).then_inc(s_z, 1)

            def pe_down(pe, b):
                t = b.t
                for slot in range(2):
                    pe.wait_ge(s_glo[slot], 4 * t + 4)
                for s in range(TILES):
                    terms = [(g[:, kc, s * P:(s + 1) * P], w[:, kc, :]) for kc in range(KC)
                             for g, w in ((g2hi, ffn["w3"][0]), (g2lo, ffn["w3"][0]), (g2hi, ffn["w3"][1]))]
                    for n, (l, r) in enumerate(terms):
                        last = mm(y_bank[:, s * P:(s + 1) * P], l, r, start=n == 0, stop=n == len(terms) - 1)
                last.then_inc(s_y, 1)

            def pe_body(pe, b, before, more):
                n = b.after(1)

                def transposes():
                    norm.pe(pe, n, t_bank)

                pe_hidden(pe, b, False, transposes if more else None)
                if before:
                    pe_down(pe, b.after(-1))
                if more:
                    pe_gates(pe, n)
                pe_hidden(pe, b, True)

            def pe_program(pe):
                if x_before is not None:
                    pe.wait_ge(x_before, BLOCKS)
                pe.wait_ge(ffn["s_lo"], ffn["n"])
                norm.pe(pe, Block(0, 0), t_bank)
                pe_gates(pe, Block(0, 0))
                run_odd(pe, pe_body)
                pe.wait_ge(s_ys, BLOCKS - 1)
                pe_down(pe, Block(BLOCKS // 2 - 1, 1))

            def act_xhi(act, n):
                act.wait_ge(norm.read, n.t + 1)
                nc.scalar.activation(xhi[n.odd][:, :], t_bank[:, :], ACT.Copy).then_inc(s_xhi, 1)

            def act_tanh(act, n):
                for c in range(KC):
                    act.wait_ge(s_ab, KC * n.t + c + 1)
                    act.wait_ge(s_hf[c % 2], 2 * n.t + c // 2)
                    nc.scalar.activation(th[c % 2][:, :], a_bank[c % 2][:, :], ACT.Tanh,
                                         scale=sc[:, 0, c:c + 1]).then_inc(s_th, 1)

            def act_gelu(act, b, second, middle=None):
                hi = g2hi if second else g1hi
                for c in range(KC):
                    if c == 2 and middle:
                        middle()
                    act.wait_ge(s_z, 2 * KC * b.t + KC * second + c + 1)
                    act.wait_ge(s_glo[c % 2], 4 * b.t + 2 * second + c // 2)
                    scale = col("h2s" if second else "h1s", c)
                    nc.scalar.activation(gf[c % 2][:, :], z_bank[c % 2], ACT.Gelu, scale=scale).then_inc(s_gf, 1)
                    nc.scalar.activation(hi[:, c, :], z_bank[c % 2], ACT.Gelu, scale=scale).then_inc(s_ghi[c % 2], 1)

            def act_body(act, b, before, more):
                n = b.after(1)
                act_gelu(act, b, False)
                if more:
                    act_xhi(act, n)
                    act_tanh(act, n)
                act_gelu(act, b, True)

            def act_program(act):
                act_xhi(act, Block(0, 0))
                act.wait_ge(ffn["s_sc"], 2)
                nc.scalar.preload_act_table(ACT.Gelu)
                act_tanh(act, Block(0, 0))
                run_odd(act, act_body)

            def dve_xlo(dve, n):
                dve.wait_ge(s_xhi, n.t + 1)
                nc.vector.tensor_tensor(xlo[n.odd][:, :], t_bank[:, :], xhi[n.odd][:, :].bitcast(F32),
                                        ALU.subtract).then_inc(s_xlo, 1)

            def dve_gates(dve, n):
                t = n.t
                for c in range(KC):
                    slot = c % 2
                    dve.wait_ge(s_th, KC * t + c + 1)
                    nc.vector.scalar_tensor_tensor(out=uu[slot][:, :], in0=th[slot][:, :], scalar=1.0,
                                                   in1=a_bank[slot][:, :], op0=ALU.add, op1=ALU.mult).then_inc(s_u, 1)
                    dve.wait_ge(s_u, KC * t + c + 1)
                    dve.wait_ge(s_hlo[slot], 2 * t + c // 2)
                    nc.vector.scalar_tensor_tensor(out=hf[slot][:, :], in0=b_bank[slot][:, :], scalar=sc[:, 1, c:c + 1],
                                                   in1=uu[slot][:, :], op0=ALU.mult, op1=ALU.mult).then_inc(s_hf[slot], 1)
                    dve.wait_ge(s_hf[slot], 2 * t + c // 2 + 1)
                    nc.vector.tensor_copy(hhi[:, c, :], hf[slot][:, :]).then_inc(s_hhi, 1)

            def dve_down(dve, b):
                dve.wait_ge(s_y, b.t + 1)
                nc.vector.tensor_tensor(y[:, :, :], tiles_of(y_bank), row4("w3s"), ALU.mult).then_inc(s_ys, 1)
                dve.wait_ge(s_ys, b.t + 1)
                nc.vector.tensor_tensor(xblk(b.t), y[:, :, :], xblk(b.t), ALU.add).then_inc(s_done, 1)

            def dve_body(dve, b, before, more):
                n = b.after(1)
                if more:
                    norm.dve(dve, n, False)
                    dve_xlo(dve, n)
                if before:
                    dve_down(dve, b.after(-1))
                if more:
                    dve_gates(dve, n)

            def dve_program(dve):
                if x_before is not None:
                    dve.wait_ge(x_before, BLOCKS)
                else:
                    dve.wait_ge(s_x0, 16)
                    dve.wait_ge(s_x1, 16)
                norm.dve(dve, Block(0, 0), True)
                dve_xlo(dve, Block(0, 0))
                dve.wait_ge(s_in, 32)
                dve_gates(dve, Block(0, 0))
                run_odd(dve, dve_body)
                dve.wait_ge(s_done, BLOCKS - 1)
                dve_down(dve, Block(BLOCKS // 2 - 1, 1))

            def pool_hlo(pool, n):
                for c in range(KC):
                    pool.wait_ge(s_hhi, KC * n.t + c + 1)
                    nc.gpsimd.tensor_tensor(hlo[:, c, :], hf[c % 2][:, :], hhi[:, c, :].bitcast(F32),
                                            ALU.subtract).then_inc(s_hlo[c % 2], 1)

            def pool_glo(pool, b, second):
                hi, lo = (g2hi, g2lo) if second else (g1hi, g1lo)
                for c in range(KC):
                    pool.wait_ge(s_gf, 2 * KC * b.t + KC * second + c + 1)
                    pool.wait_ge(s_ghi[c % 2], 4 * b.t + 2 * second + c // 2 + 1)
                    nc.gpsimd.tensor_tensor(lo[:, c, :], gf[c % 2][:, :], hi[:, c, :].bitcast(F32),
                                            ALU.subtract).then_inc(s_glo[c % 2], 1)

            def pool_body(pool, b, before, more):
                n = b.after(1)
                if more:
                    norm.pool(pool, n)
                pool_glo(pool, b, False)
                if more:
                    pool_hlo(pool, n)
                pool_glo(pool, b, True)

            def pool_program(pool):
                norm.pool(pool, Block(0, 0))
                pool_hlo(pool, Block(0, 0))
                run_odd(pool, pool_body)

            return Stage(done=s_done, sp=[], act=[act_program], dve=[dve_program], pool=[pool_program],
                                   pe=[pe_program])

        def attention_b(x_before):
            wB = sb("wB", [P, 4, E])
            WQ, WK, WV, WO = range(4)
            REP = 2 * DB
            ident_b = sb("b_ident", [P, P], BF16)
            mask = sb("b_mask", [P, GROUPS, P], BF16)
            qs = [sb(f"b_queries{i}", [P, GROUPS, TOK], F32R) for i in range(2)]
            kz = [sb(f"b_keys{i}", [P, HB, TOK], F32R) for i in range(2)]
            va = [sb(f"b_values{i}", [P, TILES, HB, REP]) for i in range(2)]
            split = {k: sb(f"b_{k}", [P, TOK], F32R) for k in ("q_hi", "q_lo", "k_hi", "k_lo")}
            prob = [sb(f"b_prob{i}", [P, 3, P]) for i in range(2 * GROUPS)]
            seg = sb("b_segment_max", [P, GROUPS, SEQS, 3 * GROUPS])
            mx = sb("b_max", [P, TILES, GROUPS, GROUPS])
            nmT = sb("b_negative_max", [HB, TOK], F32R)
            o_sb = sb("b_o", [P, GROUPS, TOK])
            oT = sb("b_oT", [P, TOK])
            den = sb("b_den", [P, TOK])
            constant_rows = (oT[0:DB, :], den[0:DB, :])
            inv = sb("b_inv", [P, TOK])
            oTn = sb("b_oTn", [P, TOK])

            SLOTS = QUART // DB
            q_dram = [nc.dram_tensor(f"b_q_dram{i}", (HB, SLOTS, DB, TOK), F32) for i in range(2)]
            k_dram = [nc.dram_tensor(f"b_k_dram{i}", (HB, SLOTS, DB, TOK), F32) for i in range(2)]
            o_dram = nc.dram_tensor("b_o_dram", (GROUPS, P, TOK), F32)

            first_pass = banks3
            second_pass = banks[0:2]
            o_bank = banks[2:4]
            misc = banks[4]

            norm = Norm("b")
            s_w = sem("b_weights_loaded")
            s_c = sem("b_constants_ready")
            s_cp = sem("b_masks_ready")
            s_i = sem("b_constant_rows_stored")
            s_xT = sem("b_xnT_ready")
            s_q, s_k, s_v = sem("b_q_product"), sem("b_k_product"), sem("b_v_product")
            s_hi, s_lo, s_vr = sem("b_hi_ready"), sem("b_lo_ready"), sem("b_v_ready")
            s_st = [sem(f"b_rows_stored{i}") for i in range(2)]
            s_ld = [[sem(f"b_rows_loaded{g}_{i}") for i in range(2)] for g in range(GROUPS)]
            s_p1 = sem("b_first_scores")
            s_red = sem("b_segments_reduced")
            s_mx = sem("b_max_ready")
            s_mt = sem("b_max_transposed")
            s_nm = sem("b_negative_max_ready")
            s_ml = [sem(f"b_max_rows_loaded{i}") for i in range(2)]
            s_p2 = sem("b_second_scores")
            s_ex = sem("b_exponentials")
            s_ms = sem("b_masked")
            s_turn = sem("b_mask_turn")
            s_pv = [sem(f"b_values_weighted{i}") for i in range(2)]
            s_oc = [sem(f"b_output_copied{i}") for i in range(2)]
            s_os = sem("b_output_stored")
            s_ol = sem("b_output_loaded")
            s_inv = sem("b_inverse_denominator")
            s_on = sem("b_output_normalised")
            s_y = sem("b_projected")
            s_bo = sem("b_bias_added_to_x")
            s_done = sem("b_x_updated")
            UNITS = SEQS * HB
            STEPS = SEQS * GROUPS
            LOADS = 16 * (1 + GROUPS)
            P1_AT = {(0, 0): 0, (0, 1): 1, (1, 0): 2, (2, 0): 3, (2, 1): 4, (3, 0): 5, (4, 0): 6, (5, 0): 7}

            def group(n):
                return n // SEQS, n % SEQS

            def pe_T(pe, n):
                wait(pe, s_nm, n.t - 1)
                norm.pe(pe, n, misc)

            def pe_q(pe, n):
                pe.wait_ge(s_xT, n.t + 1)
                project(misc, wB[:, WQ, :], xnT[n.odd][:, :]).then_inc(s_q, 1)

            def pe_k(pe, n):
                pe.wait_ge(s_lo, 2 * n.t + 1)
                project(misc, wB[:, WK, :], xnT[n.odd][:, :]).then_inc(s_k, 1)

            def pe_v(pe, n, ks):
                pe.wait_ge(s_lo, ks)
                token_major(misc, xnT[n.odd], wB[:, WV, :]).then_inc(s_v, 1)

            def pe_out(pe, b):
                pe.wait_ge(s_on, b.t + 2)
                token_major(misc, oTn, wB[:, WO, :]).then_inc(s_y, 1)

            def pe_first(pe, m, n):
                g, s = group(n)
                if s == 0:
                    pe.wait_ge(s_ld[g][m.odd], LOADS * (m.pair + 1))
                pe.wait_ge(s_red, STEPS * m.t + n)
                at = s * T
                q, k = qs[m.odd], kz[m.odd][:, g * GROUPS:(g + 1) * GROUPS, :]
                mm(first_pass[:, 0, :], ident_b[:, :], mask[:, :, :], start=True, stop=False)
                mm(first_pass[:, 0, :], q[:, g, at:at + P], k[:, :, at:at + P], start=False, stop=True)
                for pair in range(2):
                    out = first_pass[:, 1 + pair, :].rearrange("p (j c k) -> p j c k", j=2, c=2)
                    mm(first_pass[:, 1 + pair, :], q[:, g, at + P:at + T], k[:, 2 * pair:2 * pair + 2, at:at + T],
                       start=True, stop=False)
                    last = mm(out[:, :, 1, :], ident_b[:, :], mask[:, 0:2, :], start=False, stop=True)
                last.then_inc(s_p1, 1)

            def pe_maxT(pe, m):
                pe.wait_ge(s_mx, 4 * (m.t + 1))
                for tile in range(TILES):
                    last = nc.tensor.transpose(misc[0:HB, tile * P:(tile + 1) * P], mx[:, tile, :, :], ident[:, :])
                last.then_inc(s_mt, 1)

            def pe_second(pe, b, n, j):
                g, s = group(n)
                u = GROUPS * n + j
                slot = j % 2
                wait(pe, s_ex, UNITS * b.t + u - 1)
                at = s * T
                k, q = kz[b.odd][:, g * GROUPS + j, :], qs[b.odd][:, g, :]
                mm(second_pass[slot][:, 0:T], k[:, at:at + P], q[:, at:at + T])
                mm(second_pass[slot][:, T:T + P], k[:, at + P:at + T], q[:, at + P:at + T]).then_inc(s_p2, 1)

            def pe_values(pe, b, n):
                g, s = group(n)
                pe.wait_ge(s_ms, UNITS * b.t + GROUPS * (n + 1))
                pe.wait_ge(s_oc[n % 2], STEPS // 2 * b.t + n // 2)
                if n == 0:
                    pe.wait_ge(s_vr, b.t + 1)
                for kc in range(2):
                    for j in range(GROUPS):
                        pr = prob[GROUPS * (n % 2) + j]
                        last = mm(o_bank[n % 2][QUART * j:QUART * j + REP, kc * P:T],
                                  va[b.odd][:, 2 * s + kc, g * GROUPS + j, :],
                                  pr[:, 2:3, :] if kc else pr[:, 0:2, :], start=kc == 0, stop=kc == 1)
                last.then_inc(s_pv[n % 2], 1)

            def pe_body(pe, b, before, one, two):
                n1, n2 = b.after(1), b.after(2)
                for n in range(STEPS):
                    if n == 0:
                        pe.wait_ge(s_ml[b.odd], 16 * GROUPS * (b.pair + 1))
                    pe_second(pe, b, n, 0)
                    pe_second(pe, b, n, 1)
                    if one and (n, 0) in P1_AT:
                        pe_first(pe, n1, P1_AT[n, 0])
                    pe_second(pe, b, n, 2)
                    pe_second(pe, b, n, 3)
                    if one and (n, 1) in P1_AT:
                        pe_first(pe, n1, P1_AT[n, 1])
                    if n:
                        pe_values(pe, b, n - 1)
                    if two and n == 0:
                        pe_T(pe, n2)
                    if two and n == 1:
                        pe_q(pe, n2)
                    if two and n == 2:
                        pe_k(pe, n2)
                    if one and n == 3:
                        pe_v(pe, n1, 2 * (b.t + 3) if two else 2 * (b.t + 2))
                    if before and n == 4:
                        if one:
                            pe.wait_ge(s_vr, b.t + 2)
                        pe_out(pe, b.after(-1))
                    if one and n == 6:
                        if before:
                            pe.wait_ge(s_done, b.t)
                        else:
                            pe.wait_ge(s_vr, b.t + 2)
                        pe_maxT(pe, n1)
                pe_values(pe, b, STEPS - 1)

            def pe_program(pe):
                pe.wait_ge(s_w, 16)
                if x_before is not None:
                    pe.wait_ge(x_before, BLOCKS)
                pe.wait_ge(s_c, 9)
                pe.wait_ge(s_cp, 4)
                pe.wait_ge(s_const, CONSTANTS)
                b0, b1 = Block(0, 0), Block(0, 1)
                for n in (b0, b1):
                    if n is b1:
                        pe.wait_ge(s_lo, 2)
                    norm.pe(pe, n, misc)
                    pe_q(pe, n)
                    pe_k(pe, n)
                pe_v(pe, b0, 4)
                for n in range(STEPS):
                    pe_first(pe, b0, n)
                pe.wait_ge(s_vr, 1)
                pe_maxT(pe, b0)
                run_two(pe, pe_body)
                pe_out(pe, Block(BLOCKS // 2 - 1, 1))

            def act_xT(act, n):
                act.wait_ge(norm.read, n.t + 1)
                nc.scalar.activation(xnT[n.odd][:, :], misc[:, :], ACT.Copy).then_inc(s_xT, 1)

            def act_hi(act, n, k):
                act.wait_ge(s_k if k else s_q, n.t + 1)
                wait(act, s_st[1 - n.odd], 96 * (n.pair + n.odd))
                nc.scalar.activation(split["k_hi" if k else "q_hi"][:, :], misc[:, :], ACT.Identity,
                                     bias=col("bk_b" if k else "bq_b")).then_inc(s_hi, 1)

            def act_exp(act, b, n, j):
                u = GROUPS * n + j
                act.wait_ge(s_p2, UNITS * b.t + u + 1)
                if j == 0:
                    act.wait_ge(s_pv[n % 2], STEPS // 2 * b.t + n // 2)
                nc.scalar.activation(prob[u % (2 * GROUPS)][:, :, :],
                                     second_pass[j % 2][:, 0:3 * P].rearrange("p (c q) -> p c q", c=3), ACT.Exp,
                                     scale=SCALE_B).then_inc(s_ex, 1)

            def act_out(act, b, n):
                g, s = group(n)
                act.wait_ge(s_pv[n % 2], STEPS // 2 * b.t + n // 2 + 1)
                if n == 0:
                    act.wait_ge(s_os, 16 * b.t)
                nc.scalar.activation(o_sb[:, g, s * T:(s + 1) * T], o_bank[n % 2][:, 0:T], ACT.Copy)\
                    .then_inc(s_oc[n % 2], 1)

            def act_max(act, m):
                act.wait_ge(s_mt, m.t + 1)
                wait(act, s_ml[1 - m.odd], 16 * GROUPS * (m.pair + m.odd))
                nc.scalar.activation(nmT[:, :], misc[0:HB, :], ACT.Copy, scale=-1.0).then_inc(s_nm, 1)
                act.wait_ge(s_nm, m.t + 1)
                act.wait_ge(s_p1, STEPS * (m.t + 1))
                for j in range(GROUPS):
                    row = QUART * j + 3 * DB
                    act.dma_start(qs[m.odd][row:row + 1, :, :].bitcast(F32),
                                  nmT[GROUPS * j:GROUPS * (j + 1), :].bitcast(F32))\
                        .then_inc(s_ml[m.odd], 16)

            def act_body(act, b, before, one, two):
                n1, n2 = b.after(1), b.after(2)
                for n in range(STEPS):
                    for j in range(GROUPS):
                        act_exp(act, b, n, j)
                    if n:
                        act_out(act, b, n - 1)
                    if two and n == 0:
                        act_xT(act, n2)
                    if two and n == 1:
                        act_hi(act, n2, 0)
                    if two and n == 2:
                        act_hi(act, n2, 1)
                    if one and n == 6:
                        act_max(act, n1)
                act_out(act, b, STEPS - 1)

            def act_program(act):
                for n in (Block(0, 0), Block(0, 1)):
                    act_xT(act, n)
                    act_hi(act, n, 0)
                    act_hi(act, n, 1)
                act_max(act, Block(0, 0))
                nc.scalar.preload_act_table(ACT.Exp)
                run_two(act, act_body)

            def dve_lo(dve, n, k):
                dve.wait_ge(s_hi, 2 * n.t + k + 1)
                hi, lo = (split[("k_" if k else "q_") + part] for part in ("hi", "lo"))
                nc.vector.scalar_tensor_tensor(out=lo[:, :], in0=misc[:, :], scalar=col("bk_b" if k else "bq_b"),
                                               in1=hi[:, :].bitcast(F32), op0=ALU.add,
                                               op1=ALU.subtract).then_inc(s_lo, 1)

            def dve_v(dve, n):
                dve.wait_ge(s_v, n.t + 1)
                nc.vector.tensor_tensor(
                    va[n.odd][:, :, :, 0:DB], misc[:, :].rearrange("p (s h d) -> p s h d", s=TILES, h=HB),
                    row4("bv_b").rearrange("p s (h d) -> p s h d", h=HB), ALU.add).then_inc(s_vr, 1)

            def dve_first(dve, m, n):
                g, s = group(n)
                dve.wait_ge(s_p1, STEPS * m.t + n + 1)
                if n == 0:
                    dve.wait_ge(s_mx, 4 * m.t)
                nc.vector.reduce_max(seg[:, g, s, :], first_pass[:, :, :].rearrange("p b (c k) -> p (b c) k", c=4),
                                     AX.X).then_inc(s_red, 1)

            def dve_max(dve, m):
                dve.wait_ge(s_red, STEPS * (m.t + 1))
                dve.wait_ge(s_mt, m.t)
                for s in range(SEQS):
                    nc.vector.tensor_copy(mx[:, 2 * s, :, :].rearrange("p j g -> p g j"),
                                          seg[:, :, s, 0:GROUPS]).then_inc(s_mx, 1)
                    nc.vector.reduce_max(mx[:, 2 * s + 1, :, :].rearrange("p j g -> p g j"),
                                         seg[:, :, s, GROUPS:].rearrange("p g (j c) -> p g j c", c=2),
                                         AX.X).then_inc(s_mx, 1)

            def dve_out(dve, b):
                dve.wait_ge(s_ol, 32 * (b.t + 1))
                nc.vector.reciprocal(inv[:, :], den[:, :]).then_inc(s_inv, 1)
                dve.wait_ge(s_inv, b.t + 1)
                nc.vector.tensor_tensor(oTn[:, :], oT[:, :], inv[:, :], ALU.mult).then_inc(s_on, 1)

            def dve_down(dve, b):
                dve.wait_ge(s_y, b.t + 1)
                dve.wait_ge(s_bo, b.t + 1)
                nc.vector.tensor_tensor(xblk(b.t), tiles_of(misc), xblk(b.t), ALU.add).then_inc(s_done, 1)

            def dve_body(dve, b, before, one, two):
                n1, n2 = b.after(1), b.after(2)
                if two:
                    norm.dve(dve, n2, False)
                for n in range(STEPS):
                    if one and (n, 0) in P1_AT:
                        dve_first(dve, n1, P1_AT[n, 0])
                    if one and (n, 1) in P1_AT:
                        dve_first(dve, n1, P1_AT[n, 1])
                    if two and n == 1:
                        dve_lo(dve, n2, 0)
                    if two and n == 2:
                        dve_lo(dve, n2, 1)
                    if one and n == 3:
                        dve_v(dve, n1)
                    if before and n == 3:
                        dve_out(dve, b.after(-1))
                    if before and n == 4:
                        dve_down(dve, b.after(-1))
                if one:
                    dve_max(dve, n1)

            def dve_program(dve):
                if x_before is not None:
                    dve.wait_ge(x_before, BLOCKS)
                nc.vector.memset(constant_rows[0], 0.0).then_inc(s_c, 1)
                nc.vector.memset(constant_rows[1], 0.0).then_inc(s_c, 1)
                for i in range(2):
                    nc.vector.memset(kz[i][:, :, :].bitcast(F32), 0.0).then_inc(s_c, 1)
                    nc.vector.memset(va[i][:, :, :, DB:], 1.0).then_inc(s_c, 1)
                dve.wait_ge(s_c, 6)
                nc.vector.memset(den[0:1, :], 1.0).then_inc(s_c, 1)
                for i in range(2):
                    nc.vector.memset(o_bank[i][:, :], 0.0).then_inc(s_c, 1)
                dve.sem_inc(s_on, 1)
                if x_before is None:
                    dve.wait_ge(s_x0, 16)
                    dve.wait_ge(s_x1, 16)
                    dve.wait_ge(s_in, 32)
                for n in (Block(0, 0), Block(0, 1)):
                    norm.dve(dve, n, n.t == 0)
                    dve_lo(dve, n, 0)
                    dve_lo(dve, n, 1)
                dve_v(dve, Block(0, 0))
                for n in range(STEPS):
                    dve_first(dve, Block(0, 0), n)
                dve_max(dve, Block(0, 0))
                run_two(dve, dve_body)
                dve_out(dve, Block(BLOCKS // 2 - 1, 1))
                dve_down(dve, Block(BLOCKS // 2 - 1, 1))

            def pool_mask(pool, b, n):
                for j in range(GROUPS):
                    u = GROUPS * n + j
                    pr = prob[u % (2 * GROUPS)][:, 0:3:2, :]
                    pool.wait_ge(s_ex, UNITS * b.t + u + 1)
                    pool.sem_inc(s_turn, 1)
                    nc.gpsimd.affine_select(out=pr, in_=pr, compare_op=ALU.is_ge, fill=0.0, base=0,
                                            pattern=[[0, 2], [1, P]], channel_multiplier=-1).then_inc(s_ms, 1)

            def pool_body(pool, b, before, one, two):
                if two:
                    norm.pool(pool, b.after(2))
                if before:
                    nc.gpsimd.tensor_tensor(xblk(b.t - 1), xblk(b.t - 1), row4("bo_b"), ALU.add).then_inc(s_bo, 1)
                for n in range(STEPS):
                    pool_mask(pool, b, n)

            def pool_program(pool):
                if x_before is not None:
                    pool.wait_ge(x_before, BLOCKS)
                nc.gpsimd.memset(ident_b[:, :], 0.0).then_inc(s_cp, 1)
                nc.gpsimd.memset(mask[:, :, :], 0.0).then_inc(s_cp, 1)
                pool.wait_ge(s_cp, 2)
                nc.gpsimd.affine_select(out=ident_b[:, :], in_=ident_b[:, :], compare_op=ALU.not_equal, fill=1.0,
                                        base=0, pattern=[[-1, P]], channel_multiplier=1).then_inc(s_cp, 1)
                nc.gpsimd.affine_select(out=mask[:, :, :], in_=mask[:, :, :], compare_op=ALU.is_ge, fill=MASKED,
                                        base=0, pattern=[[0, GROUPS], [-1, P]], channel_multiplier=1).then_inc(s_cp, 1)
                norm.pool(pool, Block(0, 0))
                norm.pool(pool, Block(0, 1))
                run_two(pool, pool_body)
                t = BLOCKS - 1
                nc.gpsimd.tensor_tensor(xblk(t), xblk(t), row4("bo_b"), ALU.add).then_inc(s_bo, 1)

            def value(sp, v):
                return v if isinstance(v, int) else sp.snap(v)

            def rows_values(sp, n):
                return {"q_lo": value(sp, 2 * n.t + 1), "k_lo": value(sp, 2 * n.t + 2),
                        "loaded": value(sp, LOADS * n.pair), "stored": value(sp, 96 * (n.pair + 1)),
                        "used": [value(sp, UNITS * (n.t - 2) + SEQS * GROUPS * (g + 1)) for g in range(GROUPS)]}

            def sp_rows(sp, n, v, fresh):
                if not fresh:
                    for g in range(GROUPS):
                        sp.wait_ge(s_ld[g][n.odd], v["loaded"])
                for name, dram, parts in (("q", q_dram, ("hi", "lo", "hi")), ("k", k_dram, ("hi", "hi", "lo"))):
                    sp.wait_ge(s_lo, v[f"{name}_lo"])
                    for c, part in enumerate(parts):
                        sp.dma_start(dram[n.odd].ap()[:, c, :, :], split[f"{name}_{part}"][:, :].bitcast(F32))\
                            .then_inc(s_st[n.odd], 16)
                sp.wait_ge(s_st[n.odd], v["stored"])
                for g in range(GROUPS):
                    if not fresh:
                        sp.wait_ge(s_p2, v["used"][g])
                    heads = slice(g * GROUPS, (g + 1) * GROUPS)
                    sp.dma_start(qs[n.odd][:, g, :].bitcast(F32),
                                 q_dram[n.odd].ap()[heads].rearrange("j c d t -> (j c d) t")).then_inc(s_ld[g][n.odd], 16)
                    for j in range(GROUPS):
                        sp.dma_start(kz[n.odd][QUART * j:QUART * (j + 1), g * GROUPS + j, :].bitcast(F32),
                                     k_dram[n.odd].ap()[g * GROUPS + j].rearrange("c d t -> (c d) t"))\
                            .then_inc(s_ld[g][n.odd], 16)

            def out_values(sp, b):
                return {"copied": value(sp, STEPS // 2 * (b.t + 1)), "stored": value(sp, 16 * (b.t + 1)),
                        "read": value(sp, b.t + 1)}

            def sp_out(sp, b, v):
                for slot in range(2):
                    sp.wait_ge(s_oc[slot], v["copied"])
                sp.dma_start(o_dram.ap().rearrange("g p t -> p g t"), o_sb[:, :, :]).then_inc(s_os, 16)
                sp.wait_ge(s_os, v["stored"])
                sp.wait_ge(s_on, v["read"])
                view = o_dram.ap().rearrange("g (j r) t -> (g j) r t", r=QUART)
                sp.dma_start(oT[:, :], view[:, 0:DB, :]).then_inc(s_ol, 16)
                sp.dma_start(den[:, :], view[:, DB:REP, :]).then_inc(s_ol, 16)

            def sp_body(sp, b, before, one, two):
                out_at = out_values(sp, b.after(-1)) if before else None
                rows_at = rows_values(sp, b.after(2)) if two else None
                if before:
                    sp_out(sp, b.after(-1), out_at)
                if two:
                    sp_rows(sp, b.after(2), rows_at, False)

            def sp_program(sp):
                if x_before is not None:
                    sp.wait_ge(x_before, BLOCKS)
                sp.dma_start(wB[:, :, :], io["wB"].rearrange("p (w e) -> p w e", e=E)).then_inc(s_w, 16)
                sp.wait_ge(s_c, 7)
                for i in range(2):
                    for which, dram in enumerate((q_dram, k_dram)):
                        for h in range(HB):
                            sp.dma_start(dram[i].ap()[h, SLOTS - 1], constant_rows[which]).then_inc(s_i, 16)
                sp.wait_ge(s_i, 16 * 4 * HB)
                sp_rows(sp, Block(0, 0), rows_values(sp, Block(0, 0)), True)
                sp_rows(sp, Block(0, 1), rows_values(sp, Block(0, 1)), True)
                run_two(sp, sp_body)
                last = Block(BLOCKS // 2 - 1, 1)
                sp_out(sp, last, out_values(sp, last))

            return Stage(done=s_done, sp=[sp_program], act=[act_program], dve=[dve_program],
                                   pool=[pool_program], pe=[pe_program])

        def run_two(engine, body):
            last = BLOCKS // 2 - 1
            body(engine, Block(0, 0), False, True, True)
            with engine.Fori(0, last - 1) as i:
                body(engine, Block(i, 1), True, True, True)
                body(engine, Block(i + 1, 0), True, True, True)
            body(engine, Block(last - 1, 1), True, True, True)
            body(engine, Block(last, 0), True, True, False)
            body(engine, Block(last, 1), True, False, False)

        def sp_load_rest(sp):
            sp.dma_start(X[:, TILES:, :], x_dram[:, TILES:, :]).then_inc(s_x1, 16)

        def sp_store(sp):
            for t in range(BLOCKS):
                sp.wait_ge(done, t + 1)
                at = slice(TILES * t, TILES * (t + 1))
                sp.dma_start(out_dram[:, at, :], X[:, at, :]).then_inc(s_out, 16)
            sp.wait_ge(s_out, 16 * BLOCKS)

        stages, done = [], None
        split = ffn_weights()
        for k, kind in enumerate(layers):
            if kind == "F" and split not in stages:
                stages.append(split)
            scope.append(ExitStack())
            stages.append(attention_a(done) if kind == "A" else attention_b(done) if kind == "B"
                          else feed_forward(f"f{k}", done))
            done = stages[-1].done
            scope.pop().close()

        block = ctx.enter_context(nc.Block())

        @block.sync
        def _(sp):
            sp_load_tables(sp)
            if layers[0] != "A":
                sp_load_rest(sp)
            for stage in stages:
                for program in stage.sp:
                    program(sp)
            sp_store(sp)

        @block.scalar
        def _(act):
            for stage in stages:
                for program in stage.act:
                    program(act)

        @block.vector
        def _(dve):
            for stage in stages:
                for program in stage.dve:
                    program(dve)

        @block.gpsimd
        def _(pool):
            pool_constants(pool)
            for stage in stages:
                for program in stage.pool:
                    program(pool)

        @block.tensor
        def _(pe):
            for stage in stages:
                for program in stage.pe:
                    program(pe)


def host_layout(d):
    f = np.float32
    a = {k: np.asarray(v) for k, v in d.items()}
    A = lambda n: a["L0_attn_a_" + n]
    Bn = lambda n: a["L0_attn_b_" + n]
    Fn = lambda n: a["L0_ffn_" + n]
    swap = np.arange(E).reshape(HA, 4, HALF_A // 2)[:, [0, 1, 3, 2]].reshape(E)
    io = {"x": A("x").reshape(B * T, E)}
    io["wA"] = np.concatenate([A("Wq"), A("Wq")[:, swap], A("Wk"), A("Wk")[:, swap], A("Wv"), A("Wo")], 1)
    chunks = lambda w: w.reshape(-1, P, w.shape[1]).transpose(1, 0, 2).reshape(P, -1)
    io["wF"] = np.concatenate([chunks(Fn(n).T) for n in ("w1_w", "w2_w", "h1_w", "h2_w", "w3_w")], 1)
    qkv = Bn("attn_w").reshape(HB, 3, DB, E).transpose(1, 0, 2, 3).reshape(3, HB * DB, E)
    io["wB"] = np.concatenate([qkv[0].T, qkv[1].T, qkv[2].T, Bn("out_w").T], 1)
    qkv_b = Bn("attn_b").reshape(HB, 3, DB).transpose(1, 0, 2).reshape(3, HB * DB)
    per = lambda v: v.reshape(KC, P).T
    feature = np.arange(E) % DA
    spatial = feature >= HALF_A
    quarter = HALF_A // 2
    io["cols"] = np.concatenate([
        per(Fn("w1_s")), per(Fn("w2_s")), per(Fn("h1_s")), per(Fn("h2_s")),
        A("bq")[:, None], A("bq")[swap][:, None], A("bk")[:, None], A("bk")[swap][:, None],
        qkv_b[0][:, None], qkv_b[1][:, None], np.broadcast_to(A("nrope_freq"), (P, 1)),
        (-(feature % quarter) / quarter).astype(f)[:, None],
        np.where(spatial, np.where(feature < HALF_A + quarter, -1, 1), 0).astype(f)[:, None],
        spatial.astype(f)[:, None]], 1)
    io["rows"] = np.broadcast_to(
        np.concatenate([A("bv"), A("bo"), Fn("w3_s"), qkv_b[2], Bn("out_b")])[None, :], (P, len(ROWS) * E))
    return {k: np.ascontiguousarray(v) for k, v in io.items()}


def kernel(**inputs):
    import concourse.bacc as bacc
    from concourse.bass_utils import run_bass_kernel_spmd

    arrays = {f"in_{k}": v for k, v in host_layout(inputs).items()}
    nc = bacc.Bacc("TRN2", target_bir_lowering=False, num_devices=1)
    io = {k[3:]: nc.dram_tensor(k, v.shape, F32, kind="ExternalInput").ap() for k, v in arrays.items()}
    io["out"] = nc.dram_tensor("y", (B * T, E), F32, kind="ExternalOutput").ap()
    build(nc, io)
    r = run_bass_kernel_spmd(nc, [arrays], core_ids=[0])
    return r.results[0]["y"].reshape(B, T, E)
```

```python
from contextlib import ExitStack

import concourse.bass as bass
import numpy as np
from concourse import mybir

F32 = mybir.dt.float32
F32R = mybir.dt.float32r
BF16 = mybir.dt.bfloat16
I32 = mybir.dt.int32
ALU = mybir.AluOpType
ACT = mybir.ActivationFunctionType
AX = mybir.AxisListType

P = 128
B, T, E = 16, 256, 128
SEQS = 2
TOK = SEQS * T
TILES = TOK // P
BLOCKS = B * T // TOK
HID = 512
KC = HID // P
WCOLS = 2 * HID + 2 * KC * HID + KC * E
HA, DA = 2, 64
HALF_A = DA // 2
BASE_FREQUENCY, MIN_L = 10000.0, 0.83
SDT_L = (BASE_FREQUENCY - MIN_L * BASE_FREQUENCY) * 2.0
ANGLE_STEP = 2.0 * np.pi / (T - 1)
BELOW_PI = 3.1415925
SCALE_A = DA**-0.5
HB, DB = 16, 8
GROUPS = 4
QUART = P // GROUPS
SCALE_B = DB**-0.5
MASKED = -1e30
EPS = 1e-5

COLS = {}
for _name, _n in (("s1", KC), ("s2", KC), ("h1s", KC), ("h2s", KC), ("bq", 1), ("bqr", 1), ("bk", 1), ("bkr", 1),
                  ("bq_b", 1), ("bk_b", 1), ("freq", 1), ("exponent", 1), ("sign", 1), ("spatial", 1)):
    COLS[_name] = (sum(n for _, n in COLS.values()), _n)
N_COLS = sum(n for _, n in COLS.values())
ROWS = ("bv", "bo", "w3s", "bv_b", "bo_b")


class Block:

    def __init__(self, pair, odd):
        self.pair, self.odd = pair, odd
        self.t = 2 * pair + odd

    def after(self, n):
        return Block(self.pair + (self.odd + n) // 2, (self.odd + n) % 2)


class Stage:

    def __init__(self, sp, act, dve, pool, pe, done=None):
        self.sp, self.act, self.dve, self.pool, self.pe, self.done = sp, act, dve, pool, pe, done


def build(nc, io, layers=("A", "F", "B", "F")):
    ctx = ExitStack()
    with ctx:
        scope = [ctx]

        def sb(name, shape, dt=F32):
            return scope[-1].enter_context(nc.sbuf_tensor(name, shape, dt))

        def sem(name):
            return ctx.enter_context(nc.semaphore(name))

        banks5 = ctx.enter_context(nc.psum_tensor("banks5", [P, 5, 512], F32))
        banks = [banks5[:, i, :] for i in range(5)]
        banks3 = ctx.enter_context(nc.psum_tensor("banks3", [P, 3, 512], F32))

        X = sb("X", [P, B * T // P, E])
        ident = sb("ident", [P, P])
        cols = sb("cols", [P, N_COLS])
        rows = sb("rows", [P, len(ROWS), E])
        stats = sb("stats", [P, TILES, 6])
        mv = sb("mv", [P, TILES, 2])
        veps = sb("veps", [P, TILES])
        rstd = sb("rstd", [P, TILES])
        xn = sb("xn", [P, TILES, E])
        eps_t = sb("eps_t", [P, TILES])
        mhalf = sb("mhalf", [P, TILES])
        xnT = [sb(f"xnT{i}", [P, TOK]) for i in range(2)]

        def col(name, i=0):
            at, _ = COLS[name]
            return cols[:, at + i:at + i + 1]

        def row4(name):
            return rows[:, ROWS.index(name):ROWS.index(name) + 1, :].to_broadcast([P, TILES, E])

        def xblk(t):
            return X[:, bass.ds(TILES * t, TILES), :]

        s_const = sem("constants_ready")
        s_in = sem("tables_loaded")
        s_x0 = sem("x_first_block_loaded")
        s_x1 = sem("x_rest_loaded")
        s_out = sem("output_stored")

        x_dram = io["x"].rearrange("(t p) e -> p t e", p=P)
        out_dram = io["out"].rearrange("(t p) e -> p t e", p=P)

        def sp_load_tables(sp):
            sp.dma_start(cols[:, :], io["cols"]).then_inc(s_in, 16)
            sp.dma_start(X[:, 0:TILES, :], x_dram[:, 0:TILES, :]).then_inc(s_x0, 16)
            sp.dma_start(rows[:, :, :], io["rows"].rearrange("p (r e) -> p r e", e=E)).then_inc(s_in, 16)

        def pool_constants(pool):
            nc.gpsimd.memset(eps_t[:, :], EPS).then_inc(s_const, 1)
            nc.gpsimd.memset(mhalf[:, :], -0.5).then_inc(s_const, 1)
            nc.gpsimd.memset(ident[:, :], 0.0).then_inc(s_const, 1)
            pool.wait_ge(s_const, 3)
            nc.gpsimd.affine_select(out=ident[:, :], in_=ident[:, :], compare_op=ALU.not_equal, fill=1.0,
                                    base=0, pattern=[[-1, P]], channel_multiplier=1).then_inc(s_const, 1)

        CONSTANTS = 4

        class Norm:

            def __init__(self, layer):
                self.stats = sem(f"{layer}_ln_stats")
                self.moments = sem(f"{layer}_ln_moments")
                self.veps = sem(f"{layer}_ln_variance_eps")
                self.rstd = sem(f"{layer}_ln_rstd")
                self.xn = sem(f"{layer}_xn_ready")
                self.read = sem(f"{layer}_xn_transposed")

            def dve(self, dve, b, first):
                self.dve_stats(dve, b)
                self.dve_apply(dve, b, first)

            def dve_stats(self, dve, b):
                t = b.t
                for s in range(TILES):
                    nc.vector.bn_stats(stats[:, s, :], X[:, bass.ds(TILES * t + s, 1), :]).then_inc(self.stats, 1)
                dve.drain()
                for s in range(TILES):
                    nc.vector.bn_aggr(mv[:, s, :], stats[:, s, :]).then_inc(self.moments, 1)

            def dve_apply(self, dve, b, first):
                t = b.t
                dve.wait_ge(self.rstd, t + 1)
                if not first:
                    dve.wait_ge(self.read, t)
                for s in range(TILES):
                    nc.vector.tensor_scalar(xn[:, s, :], X[:, bass.ds(TILES * t + s, 1), :], mv[:, s, 0:1],
                                            rstd[:, s:s + 1], ALU.subtract, ALU.mult).then_inc(self.xn, 1)

            def pool(self, pool, b):
                t = b.t
                pool.wait_ge(self.moments, TILES * (t + 1))
                nc.gpsimd.tensor_tensor(veps[:, :], mv[:, :, 1], eps_t[:, :], ALU.add).then_inc(self.veps, 1)
                pool.wait_ge(self.veps, t + 1)
                pool.wait_ge(self.xn, TILES * t)
                nc.gpsimd.tensor_tensor(rstd[:, :], veps[:, :], mhalf[:, :], ALU.pow).then_inc(self.rstd, 1)

            def pe(self, pe, b, bank):
                pe.wait_ge(self.xn, TILES * (b.t + 1))
                for s in range(TILES):
                    last = nc.tensor.transpose(bank[:, s * P:(s + 1) * P], xn[:, s, :], ident[:, :])
                last.then_inc(self.read, 1)

        def mm(out, lhsT, rhs, start=True, stop=True):
            return nc.tensor.matmul(out, lhsT, rhs, start=start, stop=stop)

        def project(bank, w, xT):
            return mm(bank[:, :], w, xT)

        def token_major(bank, xT, w):
            for s in range(TILES):
                last = mm(bank[:, s * P:(s + 1) * P], xT[:, s * P:(s + 1) * P], w)
            return last

        def tiles_of(bank):
            return bank[:, :].rearrange("p (s e) -> p s e", s=TILES)

        def wait(engine, semaphore, value):
            if not isinstance(value, int) or value > 0:
                engine.wait_ge(semaphore, value)

        def run_two(engine, body):
            last = BLOCKS // 2 - 1
            body(engine, Block(0, 0), False, True, True)
            with engine.Fori(0, last - 1) as i:
                body(engine, Block(i, 1), True, True, True)
                body(engine, Block(i + 1, 0), True, True, True)
            body(engine, Block(last - 1, 1), True, True, True)
            body(engine, Block(last, 0), True, True, False)
            body(engine, Block(last, 1), True, False, False)

        wB = sb("wB", [P, 4, E])
        ident_b = sb("b_ident", [P, P], BF16)
        mask = sb("b_mask", [P, GROUPS, P], BF16)
        SLOTS = QUART // DB
        q_dram = [nc.dram_tensor(f"b_q_dram{i}", (HB, SLOTS, DB, TOK), F32) for i in range(2)]
        k_dram = [nc.dram_tensor(f"b_k_dram{i}", (HB, SLOTS, DB, TOK), F32) for i in range(2)]
        o_dram = nc.dram_tensor("b_o_dram", (GROUPS, P, TOK), F32)
        s_wB = sem("b_weights_loaded")
        s_cp = sem("b_masks_ready")
        s_cr = sem("b_constant_rows_made")
        s_i = sem("b_constant_rows_stored")

        def pool_b_constants(pool, constant_rows):
            nc.gpsimd.memset(constant_rows[:, :, :], 0.0).then_inc(s_cr, 1)
            nc.gpsimd.memset(ident_b[:, :], 0.0).then_inc(s_cp, 1)
            nc.gpsimd.memset(mask[:, :, :], 0.0).then_inc(s_cp, 1)
            pool.wait_ge(s_cr, 1)
            nc.gpsimd.memset(constant_rows[0:1, 1, :], 1.0).then_inc(s_cr, 1)
            pool.wait_ge(s_cp, 2)
            nc.gpsimd.affine_select(out=ident_b[:, :], in_=ident_b[:, :], compare_op=ALU.not_equal, fill=1.0,
                                    base=0, pattern=[[-1, P]], channel_multiplier=1).then_inc(s_cp, 1)
            nc.gpsimd.affine_select(out=mask[:, :, :], in_=mask[:, :, :], compare_op=ALU.is_ge, fill=MASKED,
                                    base=0, pattern=[[0, GROUPS], [-1, P]], channel_multiplier=1).then_inc(s_cp, 1)

        def sp_b_constants(sp, constant_rows):
            sp.dma_start(wB[:, :, :], io["wB"].rearrange("p (w e) -> p w e", e=E)).then_inc(s_wB, 16)
            sp.wait_ge(s_cr, 2)
            for i in range(2):
                for which, dram in enumerate((q_dram, k_dram)):
                    sp.dma_start(dram[i].ap()[:, SLOTS - 1].rearrange("h d t -> d h t"),
                                 constant_rows[:, which:which + 1, :].to_broadcast([DB, HB, TOK])).then_inc(s_i, 16)

        def attention_a(x_ready_before):
            wA = sb("wA", [P, 6, E])
            WQ, WQR, WK, WKR, WV, WO = range(6)
            C = sb("cosines", [P, T])
            S = sb("sines", [P, T])
            qT = [sb(f"a_qT{i}", [P, TOK]) for i in range(2)]
            kT = [sb(f"a_kT{i}", [P, TOK]) for i in range(2)]
            v = [sb(f"a_v{i}", [P, TILES, E]) for i in range(2)]
            turned = sb("a_turned", [P, TOK])
            straight = sb("a_straight", [P, TOK])
            prob = [sb(f"a_prob{i}", [P, 2, T]) for i in range(2)]
            probT = [sb(f"a_probT{i}", [P, 2, T]) for i in range(2)]
            mx = [sb(f"a_mx{i}", [P, 2]) for i in range(2)]
            nm = [sb(f"a_nm{i}", [P, 2]) for i in range(2)]
            total = [sb(f"a_total{i}", [P, 2]) for i in range(2)]
            inv = [sb(f"a_inv{i}", [P, 2]) for i in range(2)]
            oT = sb("a_oT", [P, TOK])
            tab = [sb(f"a_tab{i}", [P, T]) for i in range(4)]
            tcol = sb("a_tcol", [P, 8])
            posi = sb("a_posi", [P, T], I32)
            constant_rows = sb("b_constant_rows", [DB, 2, TOK])

            misc = banks[0:2]
            score = banks[2:4]
            pT_bank = [banks[4], banks3[:, 0, :]]
            o_bank = banks3[:, 1, :]
            y_bank = banks3[:, 2, :]

            norm = Norm("a")
            s_w = sem("a_weights_loaded")
            s_tab = sem("a_table_steps_pool")
            s_tabd = sem("a_table_steps_dve")
            s_taba = sem("a_table_steps_act")
            s_tr = sem("a_rope_tables_ready")
            s_xT = sem("a_xnT_ready")
            s_q = sem("a_q_product")
            s_qr = sem("a_q_rotated_product")
            s_k = sem("a_k_product")
            s_kr = sem("a_k_rotated_product")
            s_v = sem("a_v_product")
            s_st = sem("a_rope_straight")
            s_tu = sem("a_rope_turned")
            s_ro = sem("a_rope_added")
            s_vr = sem("a_v_ready")
            s_sc = sem("a_scores")
            s_mx = sem("a_max")
            s_nm = sem("a_negative_max")
            s_ex = sem("a_exponentials")
            s_in_ = sem("a_inverse_total")
            s_no = sem("a_probabilities_normalised")
            s_pt = sem("a_probabilities_transposed")
            s_pc = sem("a_probabilities_copied")
            s_pv = sem("a_values_weighted")
            s_oc = sem("a_outputs_copied")
            s_y = sem("a_projected")
            s_bo = sem("a_bias_added_to_x")
            s_done = sem("a_x_updated")

            def sp_program(sp):
                sp.dma_start(wA[:, :, :], io["wA"].rearrange("p (w e) -> p w e", e=E)).then_inc(s_w, 16)
                sp.dma_start(X[:, TILES:, :], x_dram[:, TILES:, :]).then_inc(s_x1, 16)
                sp_b_constants(sp, constant_rows)

            UNITS = SEQS * HA

            def unit(n):
                return n // HA, n % HA

            def pool_tables(pool):
                nc.gpsimd.iota(posi[:, :], pattern=[[1, T]], base=0, channel_multiplier=0).then_inc(s_tab, 1)
                pool.wait_ge(s_in, 32)
                pool.wait_ge(s_tabd, 3)
                nc.gpsimd.tensor_tensor(tcol[:, 3:4], tcol[:, 2:3], col("exponent"), ALU.pow).then_inc(s_tab, 1)

            def act_tables(act):
                act.wait_ge(s_in, 32)
                nc.scalar.activation(tcol[:, 0:1], col("freq"), ACT.Exp, scale=-1.0).then_inc(s_taba, 1)
                act.wait_ge(s_tabd, 6)
                nc.scalar.activation(tab[1][:, :], tab[0][:, :], ACT.Sin).then_inc(s_taba, 1)
                nc.scalar.activation(tab[2][:, :], tab[3][:, :], ACT.Sin).then_inc(s_taba, 1)

            def dve_tables(dve):
                dve.wait_ge(s_taba, 1)
                nc.vector.tensor_scalar_add(tcol[:, 1:2], tcol[:, 0:1], 1.0).then_inc(s_tabd, 1)
                dve.wait_ge(s_tabd, 1)
                nc.vector.reciprocal(tcol[:, 4:5], tcol[:, 1:2]).then_inc(s_tabd, 1)
                dve.wait_ge(s_tabd, 2)
                nc.vector.tensor_scalar(tcol[:, 2:3], tcol[:, 4:5], SDT_L, MIN_L * BASE_FREQUENCY,
                                        ALU.mult, ALU.add).then_inc(s_tabd, 1)
                dve.wait_ge(s_tab, 2)
                nc.vector.tensor_copy(tab[1][:, :], posi[:, :]).then_inc(s_tabd, 1)
                dve.wait_ge(s_tabd, 4)
                nc.vector.tensor_scalar(tab[2][:, :], tab[1][:, :], tcol[:, 3:4], float(ANGLE_STEP / 2),
                                        ALU.mult, ALU.mult).then_inc(s_tabd, 1)
                dve.wait_ge(s_tabd, 5)
                nc.vector.tensor_scalar_min(tab[0][:, :], tab[2][:, :], BELOW_PI)
                nc.vector.tensor_scalar(tab[3][:, :], tab[2][:, :], -1.0, float(np.pi / 2),
                                        ALU.mult, ALU.add).then_inc(s_tabd, 1)
                dve.wait_ge(s_taba, 3)
                nc.vector.tensor_tensor(tab[0][:, :], tab[1][:, :], tab[2][:, :], ALU.mult).then_inc(s_tabd, 1)
                nc.vector.tensor_tensor(tab[3][:, :], tab[1][:, :], tab[1][:, :], ALU.mult).then_inc(s_tabd, 1)
                dve.wait_ge(s_tabd, 8)
                nc.vector.tensor_scalar(S[:, :], tab[0][:, :], col("sign"), 2.0, ALU.mult, ALU.mult).then_inc(s_tr, 1)
                nc.vector.tensor_scalar(tab[1][:, :], tab[3][:, :], col("spatial"), -2.0,
                                        ALU.mult, ALU.mult).then_inc(s_tabd, 1)
                dve.wait_ge(s_tabd, 9)
                nc.vector.tensor_scalar_add(C[:, :], tab[1][:, :], 1.0).then_inc(s_tr, 1)

            def pe_T(pe, n):
                pe.wait_ge(s_ro, 2 * n.t)
                norm.pe(pe, n, misc[0])

            def pe_proj(pe, n, which):
                t = n.t
                xT = xnT[n.odd][:, :]
                if which == "q":
                    pe.wait_ge(s_xT, t + 1)
                    pe.wait_ge(s_vr, t)
                    project(misc[1], wA[:, WQ, :], xT).then_inc(s_q, 1)
                elif which == "qr":
                    project(misc[0], wA[:, WQR, :], xT).then_inc(s_qr, 1)
                elif which == "k":
                    pe.wait_ge(s_st, 2 * t + 1)
                    project(misc[1], wA[:, WK, :], xT).then_inc(s_k, 1)
                elif which == "kr":
                    pe.wait_ge(s_tu, 2 * t + 1)
                    project(misc[0], wA[:, WKR, :], xT).then_inc(s_kr, 1)
                elif which == "v":
                    pe.wait_ge(s_st, 2 * t + 2)
                    token_major(misc[1], xT, wA[:, WV, :]).then_inc(s_v, 1)

            def pe_scores(pe, b, n, fresh=False):
                s, h = unit(n)
                if n or not fresh:
                    wait(pe, s_ex, UNITS * b.t + n - 1)
                if n == 0:
                    pe.wait_ge(s_ro, 2 * (b.t + 1))
                at = slice(64 * h, 64 * h + 64)
                for qt in range(2):
                    last = mm(score[n % 2][:, qt * T:(qt + 1) * T],
                              qT[b.odd][at, s * T + qt * P:s * T + (qt + 1) * P],
                              kT[b.odd][at, s * T:(s + 1) * T])
                last.then_inc(s_sc, 1)

            def pe_probT(pe, b, n):
                pe.wait_ge(s_no, UNITS * b.t + n + 1)
                if n >= 2:
                    pe.wait_ge(s_pc, UNITS * b.t + n - 1)
                for kc in range(2):
                    for qt in range(2):
                        last = nc.tensor.transpose(pT_bank[n % 2][:, kc * T + qt * P:kc * T + (qt + 1) * P],
                                                   prob[n % 2][:, qt, kc * P:(kc + 1) * P], ident[:, :])
                last.then_inc(s_pt, 1)

            def pe_pv(pe, b, n):
                s, h = unit(n)
                pe.wait_ge(s_pc, UNITS * b.t + n + 1)
                if n == 0:
                    pe.wait_ge(s_oc, b.t)
                    pe.wait_ge(s_vr, b.t + 1)
                for kc in range(2):
                    last = mm(o_bank[64 * h:64 * h + 64, s * T:(s + 1) * T],
                              v[b.odd][:, 2 * s + kc, 64 * h:64 * h + 64], probT[n % 2][:, kc, :],
                              start=kc == 0, stop=kc == 1)
                last.then_inc(s_pv, 1)

            def pe_out(pe, b):
                pe.wait_ge(s_oc, b.t + 1)
                token_major(y_bank, oT, wA[:, WO, :]).then_inc(s_y, 1)

            def pe_body(pe, b, before, one, two):
                n1, n2 = b.after(1), b.after(2)
                for n in range(UNITS):
                    if n < 2:
                        pe_scores(pe, b, n + 2)
                    elif one:
                        pe_scores(pe, n1, n - 2)
                    pe_probT(pe, b, n)
                    if n == 0 and one:
                        pe_proj(pe, n1, "k")
                        pe_proj(pe, n1, "kr")
                    if n == 0 and before:
                        pe_out(pe, b.after(-1))
                    if n == 1 and one:
                        pe_proj(pe, n1, "v")
                    if n == 3 and two:
                        pe_proj(pe, n2, "q")
                        pe_proj(pe, n2, "qr")
                    pe_pv(pe, b, n)
                    if n == 2 and two:
                        pe_T(pe, n2)

            def pe_program(pe):
                pe.wait_ge(s_const, CONSTANTS)
                pe.wait_ge(s_w, 16)
                b0, b1 = Block(0, 0), Block(0, 1)
                norm.pe(pe, b0, misc[0])
                for which in ("q", "qr", "k", "kr", "v"):
                    pe_proj(pe, b0, which)
                pe_T(pe, b1)
                pe_scores(pe, b0, 0, True)
                pe_scores(pe, b0, 1, True)
                pe_proj(pe, b1, "q")
                pe_proj(pe, b1, "qr")
                run_two(pe, pe_body)
                pe_out(pe, Block(BLOCKS // 2 - 1, 1))

            def act_xT(act, n):
                act.wait_ge(norm.read, n.t + 1)
                nc.scalar.activation(xnT[n.odd][:, :], misc[0][:, :], ACT.Copy).then_inc(s_xT, 1)

            def act_exp(act, b, n, fresh=False):
                act.wait_ge(s_nm, UNITS * b.t + n + 1)
                if n >= 2 or not fresh:
                    wait(act, s_pt, UNITS * b.t + n - 1)
                for qt in range(2):
                    last = nc.scalar.activation(prob[n % 2][:, qt, :], score[n % 2][:, qt * T:(qt + 1) * T], ACT.Exp,
                                                bias=nm[n % 2][:, qt:qt + 1], scale=SCALE_A,
                                                accum_out=total[n % 2][:, qt:qt + 1])
                last.then_inc(s_ex, 1)

            def act_probT(act, b, n):
                act.wait_ge(s_pt, UNITS * b.t + n + 1)
                if n >= 2:
                    act.wait_ge(s_pv, UNITS * b.t + n - 1)
                nc.scalar.activation(probT[n % 2][:, :, :], pT_bank[n % 2][:, :].rearrange("p (k q) -> p k q", k=2),
                                     ACT.Copy).then_inc(s_pc, 1)

            def act_out(act, b):
                act.wait_ge(s_pv, UNITS * (b.t + 1))
                nc.scalar.activation(oT[:, :], o_bank[:, :], ACT.Copy).then_inc(s_oc, 1)

            def act_body(act, b, before, one, two):
                n1, n2 = b.after(1), b.after(2)
                if before:
                    act_out(act, b.after(-1))
                for n in range(UNITS):
                    if n < 3:
                        act_exp(act, b, n + 1, not before)
                    elif one:
                        act_exp(act, n1, 0)
                    if n == 3 and two:
                        act_xT(act, n2)
                    act_probT(act, b, n)
                    if n == 1:
                        ffn["beside"]["act"](act, b)

            def act_program(act):
                act_xT(act, Block(0, 0))
                nc.scalar.preload_act_table(ACT.Exp)
                act_xT(act, Block(0, 1))
                act_exp(act, Block(0, 0), 0, True)
                run_two(act, act_body)
                act_out(act, Block(BLOCKS // 2 - 1, 1))

            def as_seqs(ap):
                return ap.rearrange("p (s t) -> p s t", s=SEQS)

            def dve_rope(dve, n, which):
                t = n.t
                k = which in ("k", "kr")
                if which in ("q", "k"):
                    dve.wait_ge(s_k if k else s_q, t + 1)
                    dve.wait_ge(s_ro, 2 * t + k)
                    nc.vector.scalar_tensor_tensor(
                        out=as_seqs(straight[:, :]), in0=as_seqs(misc[1][:, :]), scalar=col("bk" if k else "bq"),
                        in1=C[:, :].unsqueeze(1).to_broadcast([P, SEQS, T]), op0=ALU.add, op1=ALU.mult).then_inc(s_st, 1)
                else:
                    dve.wait_ge(s_kr if k else s_qr, t + 1)
                    nc.vector.scalar_tensor_tensor(
                        out=as_seqs(turned[:, :]), in0=as_seqs(misc[0][:, :]), scalar=col("bkr" if k else "bqr"),
                        in1=S[:, :].unsqueeze(1).to_broadcast([P, SEQS, T]), op0=ALU.add, op1=ALU.mult).then_inc(s_tu, 1)

            def dve_v(dve, n):
                dve.wait_ge(s_v, n.t + 1)
                nc.vector.tensor_tensor(v[n.odd][:, :, :], tiles_of(misc[1]), row4("bv"), ALU.add).then_inc(s_vr, 1)

            def dve_max(dve, b, n):
                dve.wait_ge(s_sc, UNITS * b.t + n + 1)
                nc.vector.reduce_max(mx[n % 2][:, :], score[n % 2][:, :].rearrange("p (q k) -> p q k", q=2),
                                     AX.X).then_inc(s_mx, 1)
                dve.wait_ge(s_mx, UNITS * b.t + n + 1)
                nc.vector.tensor_scalar_mul(nm[n % 2][:, :], mx[n % 2][:, :], -SCALE_A).then_inc(s_nm, 1)

            def dve_normalise(dve, b, n):
                dve.wait_ge(s_ex, UNITS * b.t + n + 1)
                nc.vector.reciprocal(inv[n % 2][:, :], total[n % 2][:, :]).then_inc(s_in_, 1)
                dve.wait_ge(s_in_, UNITS * b.t + n + 1)
                for qt in range(2):
                    last = nc.vector.tensor_scalar_mul(prob[n % 2][:, qt, :], prob[n % 2][:, qt, :],
                                                       inv[n % 2][:, qt:qt + 1])
                last.then_inc(s_no, 1)

            def dve_update(dve, b):
                dve.wait_ge(s_y, b.t + 1)
                dve.wait_ge(s_bo, b.t + 1)
                nc.vector.tensor_tensor(xblk(b.t), tiles_of(y_bank), xblk(b.t), ALU.add).then_inc(s_done, 1)

            def dve_body(dve, b, before, one, two):
                n1, n2 = b.after(1), b.after(2)
                for n in range(UNITS):
                    if n == 1 and two:
                        norm.dve_stats(dve, n2)
                    if n == 2 and two:
                        norm.dve_apply(dve, n2, False)
                    if n < 3:
                        dve_normalise(dve, b, n + 1)
                    elif one:
                        dve_normalise(dve, n1, 0)
                    if n < 2:
                        dve_max(dve, b, n + 2)
                    elif one:
                        dve_max(dve, n1, n - 2)
                    if n == 0 and one:
                        dve_rope(dve, n1, "k")
                        dve_rope(dve, n1, "kr")
                    if n == 0 and before:
                        dve_update(dve, b.after(-1))
                    if n == 1 and one:
                        dve_v(dve, n1)
                    if n == 3 and two:
                        dve_rope(dve, n2, "q")
                        dve_rope(dve, n2, "qr")
                    if n == 3:
                        ffn["beside"]["dve"](dve, b)

            def dve_program(dve):
                b0, b1 = Block(0, 0), Block(0, 1)
                dve.wait_ge(s_x0, 16)
                norm.dve(dve, b0, True)
                dve.wait_ge(s_tr, 2)
                for which in ("q", "qr", "k", "kr"):
                    dve_rope(dve, b0, which)
                dve_v(dve, b0)
                dve.wait_ge(s_x1, 16)
                norm.dve(dve, b1, False)
                dve_max(dve, b0, 0)
                dve_max(dve, b0, 1)
                dve_normalise(dve, b0, 0)
                dve_rope(dve, b1, "q")
                dve_rope(dve, b1, "qr")
                run_two(dve, dve_body)
                dve_update(dve, Block(BLOCKS // 2 - 1, 1))

            def pool_rope(pool, n, k):
                pool.wait_ge(s_st, 2 * n.t + k + 1)
                pool.wait_ge(s_tu, 2 * n.t + k + 1)
                nc.gpsimd.tensor_tensor((kT if k else qT)[n.odd][:, :], straight[:, :], turned[:, :],
                                        ALU.add).then_inc(s_ro, 1)

            def pool_body(pool, b, before, one, two):
                if one:
                    pool_rope(pool, b.after(1), 1)
                nc.gpsimd.tensor_tensor(xblk(b.t), xblk(b.t), row4("bo"), ALU.add).then_inc(s_bo, 1)
                if two:
                    norm.pool(pool, b.after(2))
                ffn["beside"]["pool"](pool, b)
                if two:
                    pool_rope(pool, b.after(2), 0)

            def pool_program(pool):
                b0, b1 = Block(0, 0), Block(0, 1)
                norm.pool(pool, b0)
                pool_b_constants(pool, constant_rows)
                pool_rope(pool, b0, 0)
                pool_rope(pool, b0, 1)
                norm.pool(pool, b1)
                pool_rope(pool, b1, 0)
                run_two(pool, pool_body)

            return Stage(done=s_done, sp=[sp_program], act=[act_tables, act_program],
                                   dve=[dve_tables, dve_program], pool=[pool_tables, pool_program], pe=[pe_program])

        ffn = {}

        def ffn_weights():
            whi = sb("whi", [P, WCOLS], F32R)
            wlo = sb("wlo", [P, WCOLS], F32R)
            piece = 704
            stage = sb("w_stage", [P, 2, piece])
            s_w = [sem(f"f_weights_loaded{i}") for i in range(2)]
            s_hi = sem("f_weights_hi")
            s_lo = sem("f_weights_lo")
            sc = sb("f_scales", [P, 2, KC])
            s_sc = sem("f_scales_ready")
            n = WCOLS // piece
            some = sb("f_lo_in_piece", [P, WCOLS // piece])
            some_row = sb("f_lo_in_row", [P, 1])
            ones = sb("f_ones", [P, 1])
            flag = sb("f_lo_anywhere", [1, 1], I32)
            s_sm = sem("f_lo_counted")
            s_cnt = sem("f_lo_summed")
            s_all = sem("f_lo_total")
            s_flag = sem("f_lo_flag_ready")

            def sp_piece(sp, b, fresh):
                if not fresh:
                    sp.wait_ge(s_sm, b.t - 1)
                sp.dma_start(stage[:, b.odd, :], io["wF"][:, bass.ds(piece * b.t, piece)]).then_inc(s_w[b.odd], 16)

            def sp_split(sp):
                sp_piece(sp, Block(0, 0), True)
                sp_piece(sp, Block(0, 1), True)
                with sp.Fori(1, n // 2) as i:
                    sp_piece(sp, Block(i, 0), False)
                    sp_piece(sp, Block(i, 1), False)

            def act_piece(act, b):
                act.wait_ge(s_w[b.odd], 16 * (b.pair + 1))
                nc.scalar.activation(whi[:, bass.ds(piece * b.t, piece)], stage[:, b.odd, :], ACT.Copy).then_inc(s_hi, 1)

            def pool_piece(pool, b):
                at = bass.ds(piece * b.t, piece)
                pool.wait_ge(s_hi, b.t + 1)
                nc.gpsimd.tensor_tensor(wlo[:, at], stage[:, b.odd, :], whi[:, at].bitcast(F32),
                                        ALU.subtract).then_inc(s_lo, 1)

            def dve_piece(dve, b):
                dve.wait_ge(s_lo, b.t + 1)
                nc.vector.tensor_scalar(stage[:, b.odd, :], wlo[:, bass.ds(piece * b.t, piece)].bitcast(F32), 0.0, None,
                                        ALU.not_equal, ALU.add, accum_out=some[:, bass.ds(b.t, 1)]).then_inc(s_sm, 1)

            def each(part):
                def program(engine):
                    for t in range(n):
                        part(engine, Block(t // 2, t % 2))
                return program

            def dve_scales(dve):
                dve.wait_ge(s_in, 32)
                s1, s2 = COLS["s1"][0], COLS["s2"][0]
                nc.vector.tensor_scalar_mul(sc[:, 0, :], cols[:, s1:s1 + KC], 0.5).then_inc(s_sc, 1)
                dve.wait_ge(s_sc, 1)
                nc.vector.tensor_tensor(sc[:, 1, :], sc[:, 0, :], cols[:, s2:s2 + KC], ALU.mult).then_inc(s_sc, 1)
                nc.vector.memset(ones[:, :], 1.0).then_inc(s_sc, 1)

            def dve_total(dve):
                dve.wait_ge(s_sm, n)
                nc.vector.reduce_sum(some_row[:, :], some[:, :], AX.X).then_inc(s_cnt, 1)
                dve.wait_ge(s_all, 1)
                nc.vector.tensor_copy(flag[:, :], banks[0][0:1, 0:1]).then_inc(s_flag, 1)

            def pe_total(pe):
                pe.wait_ge(s_cnt, 1)
                pe.wait_ge(s_sc, 3)
                mm(banks[0][0:1, 0:1], some_row[:, :], ones[:, :]).then_inc(s_all, 1)

            ffn["beside"] = {"act": act_piece, "dve": dve_piece, "pool": pool_piece}
            ffn.update(flag=flag, s_flag=s_flag, whi=whi, wlo=wlo, s_lo=s_lo, n=n, sc=sc, s_sc=s_sc)
            at = 0
            for name, k, m in (("w1", 1, HID), ("w2", 1, HID), ("h1", KC, HID), ("h2", KC, HID), ("w3", KC, E)):
                ffn[name] = [w[:, at:at + k * m].rearrange("p (k m) -> p k m", k=k) for w in (whi, wlo)]
                at += k * m
            alone = layers[0] != "A"
            return (Stage(sp=[sp_split], act=[each(act_piece)] if alone else [],
                          dve=[dve_scales] + ([each(dve_piece)] if alone else []),
                          pool=[each(pool_piece)] if alone else [], pe=[]),
                    Stage(sp=[], act=[], dve=[dve_total], pool=[], pe=[pe_total]))

        def feed_forward(layer, x_before):
            F = layer
            ffn["xn"] = [[sb(f"{F}_xn_{part}{i}", [P, TOK], F32R) for i in range(2)] for part in ("hi", "lo")]
            ffn["h"] = [[sb(f"{F}_h_{part}{i}", [P, KC, TOK], F32R) for i in range(2)] for part in ("hi", "lo")]
            ffn["g1"] = [sb(f"{F}_g1_{part}", [P, KC, TOK], F32R) for part in ("hi", "lo")]
            ffn["g2"] = [sb(f"{F}_g2_{part}", [P, KC, TOK], F32R) for part in ("hi", "lo")]
            ffn["th"] = [sb(f"{F}_tanh{i}", [P, TOK]) for i in range(2)]
            ffn["u"] = [sb(f"{F}_gate{i}", [P, TOK]) for i in range(2)]
            ffn["hf"] = [sb(f"{F}_hidden{i}", [P, TOK]) for i in range(2)]
            ffn["gf"] = [sb(f"{F}_gelu{i}", [P, TOK]) for i in range(2)]
            ffn["y"] = sb(f"{F}_y", [P, TILES, E])
            norm = Norm(F)
            xhi, xlo = ffn["xn"]
            hhi, hlo = ffn["h"]
            g1hi, g1lo = ffn["g1"]
            g2hi, g2lo = ffn["g2"]
            th, uu, hf, gf, y, sc = (ffn[k] for k in ("th", "u", "hf", "gf", "y", "sc"))
            t_bank = banks[0]
            a_bank, b_bank = banks[1:3], banks[3:5]
            z_bank = [banks3[:, 0, :], banks3[:, 1, :]]
            y_bank = banks3[:, 2, :]
            s_xhi = sem(f"{F}_xn_hi")
            s_xlo = sem(f"{F}_xn_lo")
            s_ab = sem(f"{F}_gate_products")
            s_th = sem(f"{F}_tanh")
            s_u = sem(f"{F}_gate")
            s_hf = [sem(f"{F}_hidden{i}") for i in range(2)]
            s_hhi = sem(f"{F}_hidden_hi")
            s_hlo = [sem(f"{F}_hidden_lo{i}") for i in range(2)]
            s_z = sem(f"{F}_products")
            s_gf = sem(f"{F}_gelu")
            s_ghi = [sem(f"{F}_gelu_hi{i}") for i in range(2)]
            s_glo = [sem(f"{F}_gelu_lo{i}") for i in range(2)]
            s_y = sem(f"{F}_projected")
            s_ys = sem(f"{F}_scaled")
            s_done = sem(f"{F}_x_updated")

            GENERAL = ((0, 0), (0, 1), (1, 0))
            WHOLE = ((0, 0), (0, 1))

            def product(out, w, x, kcs, sl, parts):
                terms = [(w[i][:, kc, sl], x[j][kc]) for kc in range(kcs) for i, j in parts]
                for n, (l, r) in enumerate(terms):
                    last = mm(out, l, r, start=n == 0, stop=n == len(terms) - 1)
                return last

            def pe_gate(pe, n, c, parts):
                t = n.t
                if c == 0:
                    pe.wait_ge(s_xlo, t + 1)
                    pe.wait_ge(s_xhi, t + 1)
                x = [[xhi[n.odd][:, :]], [xlo[n.odd][:, :]]]
                if c >= 2:
                    pe.wait_ge(s_hf[c % 2], 2 * t + c // 2)
                sl = slice(c * P, (c + 1) * P)
                product(a_bank[c % 2][:, :], ffn["w1"], x, 1, sl, parts)
                product(b_bank[c % 2][:, :], ffn["w2"], x, 1, sl, parts).then_inc(s_ab, 1)

            def pe_hidden(pe, b, second, parts, beside=None):
                t = b.t
                x = (g1hi, g1lo) if second else (hhi[b.odd], hlo[b.odd])
                w = ffn["h2" if second else "h1"]
                ready = s_glo if second else s_hlo
                for slot in range(2):
                    pe.wait_ge(ready[slot], 4 * t + 2 if second else 2 * t + 2)
                x = [[x[j][:, kc, :] for kc in range(KC)] for j in range(2)]
                for c in range(KC):
                    pe.wait_ge(s_ghi[c % 2], 4 * t + 2 * second + c // 2)
                    product(z_bank[c % 2], w, x, KC, slice(c * P, (c + 1) * P), parts)\
                        .then_inc(s_z, 1)
                    if beside:
                        beside(c)

            def pe_down(pe, b, parts):
                t = b.t
                for slot in range(2):
                    pe.wait_ge(s_glo[slot], 4 * t + 4)
                for s in range(TILES):
                    terms = [((g2hi, g2lo)[j][:, kc, s * P:(s + 1) * P], ffn["w3"][i][:, kc, :]) for kc in range(KC)
                             for i, j in parts]
                    for n, (l, r) in enumerate(terms):
                        last = mm(y_bank[:, s * P:(s + 1) * P], l, r, start=n == 0, stop=n == len(terms) - 1)
                last.then_inc(s_y, 1)

            def pe_blocks(pe, parts):
                def body(pe, b, before, one, two):
                    n1, n2 = b.after(1), b.after(2)
                    pe_hidden(pe, b, False, parts, (lambda c: pe_gate(pe, n1, c, parts)) if one else None)
                    if before:
                        if not one:
                            pe.wait_ge(s_ys, b.t - 1)
                        pe_down(pe, b.after(-1), parts)
                    pe_hidden(pe, b, True, parts, (lambda c: norm.pe(pe, n2, t_bank) if c == 2 else None) if two else None)

                for c in range(KC):
                    pe_gate(pe, Block(0, 0), c, parts)
                norm.pe(pe, Block(0, 1), t_bank)
                run_two(pe, body)
                pe.wait_ge(s_ys, BLOCKS - 1)
                pe_down(pe, Block(BLOCKS // 2 - 1, 1), parts)

            def pe_program(pe):
                if x_before is not None:
                    pe.wait_ge(x_before, BLOCKS)
                pe.wait_ge(ffn["s_lo"], ffn["n"])
                pe.wait_ge(ffn["s_flag"], 1)
                norm.pe(pe, Block(0, 0), t_bank)
                with pe.If(pe.value_load(ffn["flag"][0:1, 0:1], min_val=0, max_val=P * WCOLS) > 0):
                    pe_blocks(pe, GENERAL)
                with pe.Else():
                    pe_blocks(pe, WHOLE)

            def act_xhi(act, n):
                act.wait_ge(norm.read, n.t + 1)
                nc.scalar.activation(xhi[n.odd][:, :], t_bank[:, :], ACT.Copy).then_inc(s_xhi, 1)

            def act_tanh(act, n, c):
                act.wait_ge(s_ab, KC * n.t + c + 1)
                act.wait_ge(s_hf[c % 2], 2 * n.t + c // 2)
                nc.scalar.activation(th[c % 2][:, :], a_bank[c % 2][:, :], ACT.Tanh,
                                     scale=sc[:, 0, c:c + 1]).then_inc(s_th, 1)

            def act_gelu(act, b, second, c):
                hi = g2hi if second else g1hi
                act.wait_ge(s_z, 2 * KC * b.t + KC * second + c + 1)
                act.wait_ge(s_glo[c % 2], 4 * b.t + 2 * second + c // 2)
                scale = col("h2s" if second else "h1s", c)
                nc.scalar.activation(gf[c % 2][:, :], z_bank[c % 2], ACT.Gelu, scale=scale).then_inc(s_gf, 1)
                nc.scalar.activation(hi[:, c, :], z_bank[c % 2], ACT.Gelu, scale=scale).then_inc(s_ghi[c % 2], 1)

            def act_body(act, b, before, one, two):
                n1, n2 = b.after(1), b.after(2)
                for c in range(KC):
                    act_gelu(act, b, False, c)
                    if one:
                        act_tanh(act, n1, c)
                for c in range(KC):
                    act_gelu(act, b, True, c)
                    if two and c == 2:
                        act_xhi(act, n2)

            def act_program(act):
                act_xhi(act, Block(0, 0))
                act.wait_ge(ffn["s_sc"], 2)
                nc.scalar.preload_act_table(ACT.Gelu)
                for c in range(KC):
                    act_tanh(act, Block(0, 0), c)
                act_xhi(act, Block(0, 1))
                run_two(act, act_body)

            def dve_xlo(dve, n):
                dve.wait_ge(s_xhi, n.t + 1)
                nc.vector.tensor_tensor(xlo[n.odd][:, :], t_bank[:, :], xhi[n.odd][:, :].bitcast(F32),
                                        ALU.subtract).then_inc(s_xlo, 1)

            def dve_gates(dve, n):
                t = n.t
                for c in range(KC):
                    slot = c % 2
                    dve.wait_ge(s_th, KC * t + c + 1)
                    nc.vector.scalar_tensor_tensor(out=uu[slot][:, :], in0=th[slot][:, :], scalar=1.0,
                                                   in1=a_bank[slot][:, :], op0=ALU.add, op1=ALU.mult).then_inc(s_u, 1)
                    dve.wait_ge(s_u, KC * t + c + 1)
                    dve.wait_ge(s_hlo[slot], 2 * t + c // 2)
                    nc.vector.scalar_tensor_tensor(out=hf[slot][:, :], in0=b_bank[slot][:, :], scalar=sc[:, 1, c:c + 1],
                                                   in1=uu[slot][:, :], op0=ALU.mult, op1=ALU.mult).then_inc(s_hf[slot], 1)
                    dve.wait_ge(s_hf[slot], 2 * t + c // 2 + 1)
                    nc.vector.tensor_copy(hhi[n.odd][:, c, :], hf[slot][:, :]).then_inc(s_hhi, 1)

            def dve_down(dve, b):
                dve.wait_ge(s_y, b.t + 1)
                nc.vector.tensor_tensor(y[:, :, :], tiles_of(y_bank), row4("w3s"), ALU.mult).then_inc(s_ys, 1)
                dve.wait_ge(s_ys, b.t + 1)
                nc.vector.tensor_tensor(xblk(b.t), y[:, :, :], xblk(b.t), ALU.add).then_inc(s_done, 1)

            def dve_body(dve, b, before, one, two):
                n1, n2 = b.after(1), b.after(2)
                if one:
                    dve_gates(dve, n1)
                if before:
                    if not one:
                        dve.wait_ge(s_done, b.t - 1)
                    dve_down(dve, b.after(-1))
                if two:
                    norm.dve(dve, n2, False)
                    dve_xlo(dve, n2)

            def dve_program(dve):
                if x_before is not None:
                    dve.wait_ge(x_before, BLOCKS)
                else:
                    dve.wait_ge(s_x0, 16)
                    dve.wait_ge(s_x1, 16)
                norm.dve(dve, Block(0, 0), True)
                dve_xlo(dve, Block(0, 0))
                dve.wait_ge(s_in, 32)
                dve_gates(dve, Block(0, 0))
                norm.dve(dve, Block(0, 1), False)
                dve_xlo(dve, Block(0, 1))
                run_two(dve, dve_body)
                dve.wait_ge(s_done, BLOCKS - 1)
                dve_down(dve, Block(BLOCKS // 2 - 1, 1))

            def pool_hlo(pool, n, c):
                pool.wait_ge(s_hhi, KC * n.t + c + 1)
                nc.gpsimd.tensor_tensor(hlo[n.odd][:, c, :], hf[c % 2][:, :], hhi[n.odd][:, c, :].bitcast(F32),
                                        ALU.subtract).then_inc(s_hlo[c % 2], 1)

            def pool_glo(pool, b, second, c):
                hi, lo = (g2hi, g2lo) if second else (g1hi, g1lo)
                pool.wait_ge(s_gf, 2 * KC * b.t + KC * second + c + 1)
                pool.wait_ge(s_ghi[c % 2], 4 * b.t + 2 * second + c // 2 + 1)
                nc.gpsimd.tensor_tensor(lo[:, c, :], gf[c % 2][:, :], hi[:, c, :].bitcast(F32),
                                        ALU.subtract).then_inc(s_glo[c % 2], 1)

            def pool_body(pool, b, before, one, two):
                for c in range(KC):
                    pool_glo(pool, b, False, c)
                    if one:
                        pool_hlo(pool, b.after(1), c)
                for c in range(KC):
                    if two and c == 0:
                        norm.pool(pool, b.after(2))
                    pool_glo(pool, b, True, c)

            def pool_program(pool):
                norm.pool(pool, Block(0, 0))
                for c in range(KC):
                    pool_hlo(pool, Block(0, 0), c)
                norm.pool(pool, Block(0, 1))
                run_two(pool, pool_body)

            return Stage(done=s_done, sp=[], act=[act_program], dve=[dve_program], pool=[pool_program],
                                   pe=[pe_program])

        def attention_b(x_before):
            WQ, WK, WV, WO = range(4)
            REP = 2 * DB
            qs = [sb(f"b_queries{i}", [P, GROUPS, TOK], F32R) for i in range(2)]
            kz = [sb(f"b_keys{i}", [P, HB, TOK], F32R) for i in range(2)]
            va = [sb(f"b_values{i}", [P, TILES, HB, REP]) for i in range(2)]
            split = {k: sb(f"b_{k}", [P, TOK], F32R) for k in ("q_hi", "q_lo", "k_hi", "k_lo")}
            prob = [sb(f"b_prob{i}", [P, 3, P]) for i in range(2 * GROUPS)]
            seg = sb("b_segment_max", [P, GROUPS, SEQS, 3 * GROUPS])
            mx = sb("b_max", [P, TILES, GROUPS, GROUPS])
            nmT = sb("b_negative_max", [HB, TOK], F32R)
            o_sb = sb("b_o", [P, GROUPS, TOK])
            oT = sb("b_oT", [P, TOK])
            den = sb("b_den", [P, TOK])
            inv = sb("b_inv", [P, TOK])
            oTn = sb("b_oTn", [P, TOK])

            first_pass = banks3
            second_set = banks5[:, 0:3, :]
            second_pass = banks[0:2]
            o_bank = banks[2:4]
            misc = banks[4]

            norm = Norm("b")
            s_c = sem("b_buffers_filled")
            s_z0 = sem("b_keys0_zeroed")
            s_z1 = sem("b_keys1_zeroed")
            s_xT = sem("b_xnT_ready")
            s_q, s_k, s_v = sem("b_q_product"), sem("b_k_product"), sem("b_v_product")
            s_hi, s_lo, s_vr = sem("b_hi_ready"), sem("b_lo_ready"), sem("b_v_ready")
            s_st = [sem(f"b_rows_stored{i}") for i in range(2)]
            s_ld = [[sem(f"b_rows_loaded{half}_{i}") for i in range(2)] for half in range(2)]
            s_p1 = sem("b_first_scores")
            s_red = sem("b_segments_reduced")
            s_mx = sem("b_max_ready")
            s_mt = sem("b_max_transposed")
            s_nm = sem("b_negative_max_ready")
            s_ml = [sem(f"b_max_rows_loaded{i}") for i in range(2)]
            s_p2 = sem("b_second_scores")
            s_ex = sem("b_exponentials")
            s_ms = sem("b_masked")
            s_turn = sem("b_mask_turn")
            s_pv = [sem(f"b_values_weighted{i}") for i in range(2)]
            s_oc = [sem(f"b_output_copied{i}") for i in range(2)]
            s_os = sem("b_output_stored")
            s_inv = sem("b_inverse_denominator")
            s_ol = sem("b_output_loaded")
            s_on = sem("b_output_normalised")
            s_y = sem("b_projected")
            s_bo = sem("b_bias_added_to_x")
            s_done = sem("b_x_updated")
            UNITS = SEQS * HB
            STEPS = SEQS * GROUPS
            V_AT, T_AT, Q_AT, K_AT, OUT_AT = 0, 2, 3, 4, 7
            LOADS = 16 * (1 + GROUPS)
            STORES = 16 * 6
            P1_BEFORE = (0,)
            P1_AT = {(0, 1): 1, (1, 0): 2, (2, 0): 3, (2, 1): 4, (3, 0): 5, (4, 0): 6, (5, 0): 7}
            MAX_AT = 6

            def group(n):
                return n // SEQS, n % SEQS

            def pe_q(pe, n):
                pe.wait_ge(s_xT, n.t + 1)
                project(misc, wB[:, WQ, :], xnT[n.odd][:, :]).then_inc(s_q, 1)

            def pe_k(pe, n):
                pe.wait_ge(s_lo, 2 * n.t + 1)
                project(misc, wB[:, WK, :], xnT[n.odd][:, :]).then_inc(s_k, 1)

            def pe_v(pe, n):
                token_major(misc, xnT[n.odd], wB[:, WV, :]).then_inc(s_v, 1)

            def pe_out(pe, b):
                pe.wait_ge(s_on, b.t + 2)
                token_major(misc, oTn, wB[:, WO, :]).then_inc(s_y, 1)

            def pe_first(pe, m, n, first_pass=first_pass, ahead=0):
                g, s = group(n)
                if s == 0 and g % 2 == 0:
                    pe.wait_ge(s_ld[g // 2][m.odd], LOADS * (m.pair + 1))
                wait(pe, s_red, STEPS * m.t + n - ahead)
                at = s * T
                q, k = qs[m.odd], kz[m.odd][:, g * GROUPS:(g + 1) * GROUPS, :]
                mm(first_pass[:, 0, :], ident_b[:, :], mask[:, :, :], start=True, stop=False)
                mm(first_pass[:, 0, :], q[:, g, at:at + P], k[:, :, at:at + P], start=False, stop=True)
                for pair in range(2):
                    out = first_pass[:, 1 + pair, :].rearrange("p (j c k) -> p j c k", j=2, c=2)
                    mm(first_pass[:, 1 + pair, :], q[:, g, at + P:at + T], k[:, 2 * pair:2 * pair + 2, at:at + T],
                       start=True, stop=False)
                    last = mm(out[:, :, 1, :], ident_b[:, :], mask[:, 0:2, :], start=False, stop=True)
                last.then_inc(s_p1, 1)

            def pe_maxT(pe, m):
                pe.wait_ge(s_mx, 4 * (m.t + 1))
                for tile in range(TILES):
                    last = nc.tensor.transpose(misc[0:HB, tile * P:(tile + 1) * P], mx[:, tile, :, :], ident[:, :])
                last.then_inc(s_mt, 1)

            def pe_second(pe, b, n, j):
                g, s = group(n)
                u = GROUPS * n + j
                slot = j % 2
                wait(pe, s_ex, UNITS * b.t + u - 1)
                at = s * T
                k, q = kz[b.odd][:, g * GROUPS + j, :], qs[b.odd][:, g, :]
                mm(second_pass[slot][:, 0:T], k[:, at:at + P], q[:, at:at + T])
                mm(second_pass[slot][:, T:T + P], k[:, at + P:at + T], q[:, at + P:at + T]).then_inc(s_p2, 1)

            def pe_values(pe, b, n):
                g, s = group(n)
                pe.wait_ge(s_ms, UNITS * b.t + GROUPS * (n + 1))
                pe.wait_ge(s_oc[n % 2], STEPS // 2 * b.t + n // 2)
                if n == 0:
                    pe.wait_ge(s_vr, b.t + 1)
                for kc in range(2):
                    for j in range(GROUPS):
                        pr = prob[GROUPS * (n % 2) + j]
                        last = mm(o_bank[n % 2][QUART * j:QUART * j + REP, kc * P:T],
                                  va[b.odd][:, 2 * s + kc, g * GROUPS + j, :],
                                  pr[:, 2:3, :] if kc else pr[:, 0:2, :], start=kc == 0, stop=kc == 1)
                last.then_inc(s_pv[n % 2], 1)

            def pe_body(pe, b, before, one, two):
                n1, n2 = b.after(1), b.after(2)
                for n in P1_BEFORE if one else ():
                    pe_first(pe, n1, n)
                for n in range(STEPS):
                    if n == 0:
                        pe.wait_ge(s_ml[b.odd], 16 * (b.pair + 1))
                    pe_second(pe, b, n, 0)
                    pe_second(pe, b, n, 1)
                    if one and (n, 0) in P1_AT:
                        pe_first(pe, n1, P1_AT[n, 0])
                    pe_second(pe, b, n, 2)
                    pe_second(pe, b, n, 3)
                    if one and (n, 1) in P1_AT:
                        pe_first(pe, n1, P1_AT[n, 1])
                    if n:
                        pe_values(pe, b, n - 1)
                    if one and n == V_AT:
                        if before:
                            pe.wait_ge(s_nm, b.t + 1)
                        pe_v(pe, n1)
                    if two and n == T_AT:
                        pe.wait_ge(s_vr, b.t + 2)
                        norm.pe(pe, n2, misc)
                    if two and n == Q_AT:
                        pe_q(pe, n2)
                    if two and n == K_AT:
                        pe_k(pe, n2)
                    if one and n == MAX_AT:
                        if two:
                            pe.wait_ge(s_lo, 2 * (b.t + 3))
                        else:
                            pe.wait_ge(s_vr, b.t + 2)
                        pe_maxT(pe, n1)
                    if before and n == OUT_AT:
                        pe.wait_ge(s_nm, b.t + 2 if one else b.t + 1)
                        pe_out(pe, b.after(-1))
                pe_values(pe, b, STEPS - 1)

            def pe_program(pe):
                pe.wait_ge(s_wB, 16)
                if x_before is not None:
                    pe.wait_ge(x_before, BLOCKS)
                b0, b1 = Block(0, 0), Block(0, 1)
                for n in (b0, b1):
                    if n is b1:
                        pe.wait_ge(s_lo, 2)
                    norm.pe(pe, n, misc)
                    pe_q(pe, n)
                    pe_k(pe, n)
                pe.wait_ge(s_lo, 4)
                pe_v(pe, b0)
                pe.wait_ge(s_c, 4)
                pe.wait_ge(s_cp, 4)
                for n in range(STEPS):
                    pe_first(pe, b0, n, (first_pass, second_set)[n % 2], 1)
                pe.wait_ge(s_vr, 1)
                pe_maxT(pe, b0)
                run_two(pe, pe_body)
                pe_out(pe, Block(BLOCKS // 2 - 1, 1))

            def act_xT(act, n):
                act.wait_ge(norm.read, n.t + 1)
                nc.scalar.activation(xnT[n.odd][:, :], misc[:, :], ACT.Copy).then_inc(s_xT, 1)

            def act_hi(act, n, k):
                act.wait_ge(s_k if k else s_q, n.t + 1)
                wait(act, s_st[1 - n.odd], STORES * (n.pair + n.odd))
                nc.scalar.activation(split["k_hi" if k else "q_hi"][:, :], misc[:, :], ACT.Identity,
                                     bias=col("bk_b" if k else "bq_b")).then_inc(s_hi, 1)

            def act_exp(act, b, n, j):
                u = GROUPS * n + j
                act.wait_ge(s_p2, UNITS * b.t + u + 1)
                if j == 0:
                    act.wait_ge(s_pv[n % 2], STEPS // 2 * b.t + n // 2)
                nc.scalar.activation(prob[u % (2 * GROUPS)][:, :, :],
                                     second_pass[j % 2][:, 0:3 * P].rearrange("p (c q) -> p c q", c=3), ACT.Exp,
                                     scale=SCALE_B).then_inc(s_ex, 1)

            def act_out(act, b, n):
                g, s = group(n)
                act.wait_ge(s_pv[n % 2], STEPS // 2 * b.t + n // 2 + 1)
                if n == 0:
                    act.wait_ge(s_os, 16 * b.t)
                nc.scalar.activation(o_sb[:, g, s * T:(s + 1) * T], o_bank[n % 2][:, 0:T], ACT.Copy)\
                    .then_inc(s_oc[n % 2], 1)

            def act_max(act, m):
                act.wait_ge(s_mt, m.t + 1)
                wait(act, s_ml[1 - m.odd], 16 * (m.pair + m.odd))
                nc.scalar.activation(nmT[:, :], misc[0:HB, :], ACT.Copy, scale=-1.0).then_inc(s_nm, 1)
                act.wait_ge(s_nm, m.t + 1)
                act.wait_ge(s_p1, STEPS * (m.t + 1))
                act.dma_start(qs[m.odd][3 * DB::QUART, :, :].bitcast(F32), nmT[:, :].bitcast(F32))\
                    .then_inc(s_ml[m.odd], 16)

            def act_body(act, b, before, one, two):
                n1, n2 = b.after(1), b.after(2)
                for n in range(STEPS):
                    for j in range(GROUPS):
                        act_exp(act, b, n, j)
                    if n:
                        act_out(act, b, n - 1)
                    if two and n == T_AT:
                        act_xT(act, n2)
                    if two and n == Q_AT:
                        act_hi(act, n2, 0)
                    if two and n == K_AT:
                        act_hi(act, n2, 1)
                    if one and n == MAX_AT:
                        act_max(act, n1)
                act_out(act, b, STEPS - 1)

            def act_program(act):
                for n in (Block(0, 0), Block(0, 1)):
                    act_xT(act, n)
                    act_hi(act, n, 0)
                    act_hi(act, n, 1)
                act_max(act, Block(0, 0))
                nc.scalar.preload_act_table(ACT.Exp)
                run_two(act, act_body)

            def dve_lo(dve, n, k):
                dve.wait_ge(s_hi, 2 * n.t + k + 1)
                hi, lo = (split[("k_" if k else "q_") + part] for part in ("hi", "lo"))
                nc.vector.scalar_tensor_tensor(out=lo[:, :], in0=misc[:, :], scalar=col("bk_b" if k else "bq_b"),
                                               in1=hi[:, :].bitcast(F32), op0=ALU.add,
                                               op1=ALU.subtract).then_inc(s_lo, 1)

            def dve_v(dve, n):
                dve.wait_ge(s_v, n.t + 1)
                nc.vector.tensor_tensor(
                    va[n.odd][:, :, :, 0:DB], misc[:, :].rearrange("p (s h d) -> p s h d", s=TILES, h=HB),
                    row4("bv_b").rearrange("p s (h d) -> p s h d", h=HB), ALU.add).then_inc(s_vr, 1)

            def dve_first(dve, m, n, banks=first_pass):
                g, s = group(n)
                dve.wait_ge(s_p1, STEPS * m.t + n + 1)
                if n == 0:
                    dve.wait_ge(s_mx, 4 * m.t)
                nc.vector.reduce_max(seg[:, g, s, :], banks[:, :, :].rearrange("p b (c k) -> p (b c) k", c=4),
                                     AX.X).then_inc(s_red, 1)

            def dve_max(dve, m):
                dve.wait_ge(s_red, STEPS * (m.t + 1))
                dve.wait_ge(s_mt, m.t)
                for s in range(SEQS):
                    nc.vector.tensor_copy(mx[:, 2 * s, :, :].rearrange("p j g -> p g j"),
                                          seg[:, :, s, 0:GROUPS]).then_inc(s_mx, 1)
                    nc.vector.reduce_max(mx[:, 2 * s + 1, :, :].rearrange("p j g -> p g j"),
                                         seg[:, :, s, GROUPS:].rearrange("p g (j c) -> p g j c", c=2),
                                         AX.X).then_inc(s_mx, 1)

            def dve_out(dve, b):
                dve.wait_ge(s_ol, 32 * (b.t + 1))
                nc.vector.reciprocal(inv[:, :], den[:, :]).then_inc(s_inv, 1)
                dve.wait_ge(s_inv, b.t + 1)
                nc.vector.tensor_tensor(oTn[:, :], oT[:, :], inv[:, :], ALU.mult).then_inc(s_on, 1)

            def dve_down(dve, b):
                dve.wait_ge(s_y, b.t + 1)
                dve.wait_ge(s_bo, b.t + 1)
                nc.vector.tensor_tensor(xblk(b.t), tiles_of(misc), xblk(b.t), ALU.add).then_inc(s_done, 1)

            def dve_body(dve, b, before, one, two):
                n1, n2 = b.after(1), b.after(2)
                for n in P1_BEFORE if one else ():
                    dve_first(dve, n1, n)
                for n in range(STEPS):
                    if two and n == T_AT:
                        norm.dve_apply(dve, n2, False)
                    if one and (n, 0) in P1_AT:
                        dve_first(dve, n1, P1_AT[n, 0])
                    if one and (n, 1) in P1_AT:
                        dve_first(dve, n1, P1_AT[n, 1])
                    if two and n == 0:
                        norm.dve_stats(dve, n2)
                    if one and n == V_AT:
                        dve_v(dve, n1)
                    if two and n == Q_AT:
                        dve_lo(dve, n2, 0)
                    if two and n == K_AT:
                        dve_lo(dve, n2, 1)
                    if one and n == MAX_AT:
                        dve_max(dve, n1)
                    if before and n == OUT_AT - 1:
                        dve_out(dve, b.after(-1))
                    if before and n == OUT_AT:
                        dve_down(dve, b.after(-1))

            def dve_program(dve):
                if x_before is not None:
                    dve.wait_ge(x_before, BLOCKS)
                b0, b1 = Block(0, 0), Block(0, 1)
                norm.dve(dve, b0, True)
                dve.sem_inc(s_on, 1)
                for i in range(2):
                    nc.vector.memset(va[i][:, :, :, DB:], 1.0).then_inc(s_c, 1)
                    nc.vector.memset(o_bank[i][:, :], 0.0).then_inc(s_c, 1)
                dve_lo(dve, b0, 0)
                dve_lo(dve, b0, 1)
                norm.dve(dve, b1, False)
                nc.vector.memset(kz[0][:, :, :].bitcast(F32), 0.0).then_inc(s_z0, 1)
                dve_lo(dve, b1, 0)
                dve_lo(dve, b1, 1)
                dve_v(dve, b0)
                for n in range(STEPS):
                    dve_first(dve, b0, n, (first_pass, second_set)[n % 2])
                dve_max(dve, b0)
                run_two(dve, dve_body)
                dve_out(dve, Block(BLOCKS // 2 - 1, 1))
                dve_down(dve, Block(BLOCKS // 2 - 1, 1))

            def pool_mask(pool, b, n):
                for j in range(GROUPS):
                    u = GROUPS * n + j
                    pr = prob[u % (2 * GROUPS)][:, 0:3:2, :]
                    pool.wait_ge(s_ex, UNITS * b.t + u + 1)
                    pool.sem_inc(s_turn, 1)
                    nc.gpsimd.affine_select(out=pr, in_=pr, compare_op=ALU.is_ge, fill=0.0, base=0,
                                            pattern=[[0, 2], [1, P]], channel_multiplier=-1).then_inc(s_ms, 1)

            def pool_body(pool, b, before, one, two):
                for n in range(STEPS):
                    pool_mask(pool, b, n)
                    if two and n == 0:
                        norm.pool(pool, b.after(2))
                    if before and n == 1:
                        nc.gpsimd.tensor_tensor(xblk(b.t - 1), xblk(b.t - 1), row4("bo_b"), ALU.add).then_inc(s_bo, 1)

            def pool_program(pool):
                if x_before is not None:
                    pool.wait_ge(x_before, BLOCKS)
                norm.pool(pool, Block(0, 0))
                norm.pool(pool, Block(0, 1))
                nc.gpsimd.memset(kz[1][:, :, :].bitcast(F32), 0.0).then_inc(s_z1, 1)
                run_two(pool, pool_body)
                t = BLOCKS - 1
                nc.gpsimd.tensor_tensor(xblk(t), xblk(t), row4("bo_b"), ALU.add).then_inc(s_bo, 1)

            def value(sp, v):
                return v if isinstance(v, int) else sp.snap(v)

            def rows_values(sp, n):
                return {"q_lo": value(sp, 2 * n.t + 1), "k_lo": value(sp, 2 * n.t + 2),
                        "loaded": value(sp, LOADS * n.pair), "stored": value(sp, STORES * (n.pair + 1)),
                        "used": [value(sp, UNITS * (n.t - 2) + UNITS // 2 * (half + 1)) for half in range(2)]}

            def sp_rows(sp, n, v, fresh, zeroed=None):
                if not fresh:
                    for half in range(2):
                        sp.wait_ge(s_ld[half][n.odd], v["loaded"])
                for name, dram, parts in (("q", q_dram, ("hi", "lo", "hi")), ("k", k_dram, ("hi", "hi", "lo"))):
                    sp.wait_ge(s_lo, v[f"{name}_lo"])
                    for c, part in enumerate(parts):
                        sp.dma_start(dram[n.odd].ap()[:, c, :, :], split[f"{name}_{part}"][:, :].bitcast(F32))\
                            .then_inc(s_st[n.odd], 16)
                sp.wait_ge(s_st[n.odd], v["stored"])
                if zeroed:
                    sp.wait_ge(zeroed, 1)
                for half in range(2):
                    if not fresh:
                        sp.wait_ge(s_p2, v["used"][half])
                    g = 2 * half
                    heads = slice(g * GROUPS, (g + 2) * GROUPS)
                    sp.dma_start(qs[n.odd][:, g:g + 2, :].bitcast(F32),
                                 q_dram[n.odd].ap()[heads].rearrange("(g j) c d t -> (j c d) g t", g=2))\
                        .then_inc(s_ld[half][n.odd], 16)
                    for j in range(GROUPS):
                        at = slice(g * GROUPS + j, (g + 2) * GROUPS, GROUPS)
                        sp.dma_start(kz[n.odd][QUART * j:QUART * (j + 1), at, :].bitcast(F32),
                                     k_dram[n.odd].ap()[at].rearrange("g c d t -> (c d) g t"))\
                            .then_inc(s_ld[half][n.odd], 16)

            def out_values(sp, b):
                return {"copied": value(sp, STEPS // 2 * (b.t + 1)), "stored": value(sp, 16 * (b.t + 1)),
                        "read": value(sp, b.t + 1)}

            def sp_out(sp, b, v):
                for slot in range(2):
                    sp.wait_ge(s_oc[slot], v["copied"])
                sp.dma_start(o_dram.ap().rearrange("g p t -> p g t"), o_sb[:, :, :]).then_inc(s_os, 16)
                sp.wait_ge(s_os, v["stored"])
                sp.wait_ge(s_on, v["read"])
                view = o_dram.ap().rearrange("g (j r) t -> (g j) r t", r=QUART)
                sp.dma_start(oT[:, :], view[:, 0:DB, :]).then_inc(s_ol, 16)
                sp.dma_start(den[:, :], view[:, DB:REP, :]).then_inc(s_ol, 16)

            def sp_body(sp, b, before, one, two):
                out_at = out_values(sp, b.after(-1)) if before else None
                rows_at = rows_values(sp, b.after(2)) if two else None
                if before:
                    sp_out(sp, b.after(-1), out_at)
                if two:
                    sp_rows(sp, b.after(2), rows_at, False)

            def sp_program(sp):
                if x_before is not None:
                    sp.wait_ge(x_before, BLOCKS)
                sp.wait_ge(s_i, 16 * 4)
                sp_rows(sp, Block(0, 0), rows_values(sp, Block(0, 0)), True, s_z0)
                sp_rows(sp, Block(0, 1), rows_values(sp, Block(0, 1)), True, s_z1)
                run_two(sp, sp_body)
                last = Block(BLOCKS // 2 - 1, 1)
                sp_out(sp, last, out_values(sp, last))

            return Stage(done=s_done, sp=[sp_program], act=[act_program], dve=[dve_program],
                                   pool=[pool_program], pe=[pe_program])

        def sp_load_rest(sp):
            sp.dma_start(X[:, TILES:, :], x_dram[:, TILES:, :]).then_inc(s_x1, 16)

        def sp_store(sp):
            for t in range(BLOCKS):
                sp.wait_ge(done, t + 1)
                at = slice(TILES * t, TILES * (t + 1))
                sp.dma_start(out_dram[:, at, :], X[:, at, :]).then_inc(s_out, 16)
            sp.wait_ge(s_out, 16 * BLOCKS)

        split, split_total = ffn_weights()
        stages, done = [], None
        for k, kind in enumerate(layers):
            if kind == "F" and split not in stages:
                stages += [split, split_total]
            scope.append(ExitStack())
            stages.append(attention_a(done) if kind == "A" else attention_b(done) if kind == "B"
                          else feed_forward(f"f{k}", done))
            done = stages[-1].done
            scope.pop().close()

        block = ctx.enter_context(nc.Block())

        @block.sync
        def _(sp):
            sp_load_tables(sp)
            if layers[0] != "A":
                sp_load_rest(sp)
            for stage in stages:
                for program in stage.sp:
                    program(sp)
            sp_store(sp)

        @block.scalar
        def _(act):
            for stage in stages:
                for program in stage.act:
                    program(act)

        @block.vector
        def _(dve):
            for stage in stages:
                for program in stage.dve:
                    program(dve)

        @block.gpsimd
        def _(pool):
            pool_constants(pool)
            for stage in stages:
                for program in stage.pool:
                    program(pool)

        @block.tensor
        def _(pe):
            for stage in stages:
                for program in stage.pe:
                    program(pe)


def host_layout(d):
    f = np.float32
    a = {k: np.asarray(v) for k, v in d.items()}
    A = lambda n: a["L0_attn_a_" + n]
    Bn = lambda n: a["L0_attn_b_" + n]
    Fn = lambda n: a["L0_ffn_" + n]
    swap = np.arange(E).reshape(HA, 4, HALF_A // 2)[:, [0, 1, 3, 2]].reshape(E)
    io = {"x": A("x").reshape(B * T, E)}
    io["wA"] = np.concatenate([A("Wq"), A("Wq")[:, swap], A("Wk"), A("Wk")[:, swap], A("Wv"), A("Wo")], 1)
    chunks = lambda w: w.reshape(-1, P, w.shape[1]).transpose(1, 0, 2).reshape(P, -1)
    io["wF"] = np.concatenate([chunks(Fn(n).T) for n in ("w1_w", "w2_w", "h1_w", "h2_w", "w3_w")], 1)
    qkv = Bn("attn_w").reshape(HB, 3, DB, E).transpose(1, 0, 2, 3).reshape(3, HB * DB, E)
    io["wB"] = np.concatenate([qkv[0].T, qkv[1].T, qkv[2].T, Bn("out_w").T], 1)
    qkv_b = Bn("attn_b").reshape(HB, 3, DB).transpose(1, 0, 2).reshape(3, HB * DB)
    per = lambda v: v.reshape(KC, P).T
    feature = np.arange(E) % DA
    spatial = feature >= HALF_A
    quarter = HALF_A // 2
    io["cols"] = np.concatenate([
        per(Fn("w1_s")), per(Fn("w2_s")), per(Fn("h1_s")), per(Fn("h2_s")),
        A("bq")[:, None], A("bq")[swap][:, None], A("bk")[:, None], A("bk")[swap][:, None],
        qkv_b[0][:, None], qkv_b[1][:, None], np.broadcast_to(A("nrope_freq"), (P, 1)),
        (-(feature % quarter) / quarter).astype(f)[:, None],
        np.where(spatial, np.where(feature < HALF_A + quarter, -1, 1), 0).astype(f)[:, None],
        spatial.astype(f)[:, None]], 1)
    io["rows"] = np.broadcast_to(
        np.concatenate([A("bv"), A("bo"), Fn("w3_s"), qkv_b[2], Bn("out_b")])[None, :], (P, len(ROWS) * E))
    return {k: np.ascontiguousarray(v) for k, v in io.items()}


def kernel(**inputs):
    import concourse.bacc as bacc
    from concourse.bass_utils import run_bass_kernel_spmd

    arrays = {f"in_{k}": v for k, v in host_layout(inputs).items()}
    nc = bacc.Bacc("TRN2", target_bir_lowering=False, num_devices=1)
    io = {k[3:]: nc.dram_tensor(k, v.shape, F32, kind="ExternalInput").ap() for k, v in arrays.items()}
    io["out"] = nc.dram_tensor("y", (B * T, E), F32, kind="ExternalOutput").ap()
    build(nc, io)
    r = run_bass_kernel_spmd(nc, [arrays], core_ids=[0])
    return r.results[0]["y"].reshape(B, T, E)
```
